# Optimizing a Trainium2 kernel written in Bass

```python
import numpy as np
import jax
import jax.numpy as jnp

def _softmax(x, axis=-1):
    return jax.nn.softmax(x, axis=axis)

def _gelu(x):
    return jax.nn.gelu(x, approximate=True)

def _silu(x):
    return jax.nn.silu(x)

def _sigmoid(x):
    return jax.nn.sigmoid(x)

def _layernorm(x, axis=-1, eps=1e-05):
    m = jnp.mean(x, axis=axis, keepdims=True)
    v = jnp.var(x, axis=axis, keepdims=True)
    return (x - m) / jnp.sqrt(v + eps)

def _scatter_add(tgt, idx, src, axis=0):
    return tgt.at[idx].add(src)

def _segment_sum(src, seg, n):
    return jax.ops.segment_sum(src, seg, n)
kernel_name = 'mk_xattn_ffn_d1_seqx_r4_8a5a5f'

def setup_inputs(seed: int=0):
    np.random.seed(seed)
    _w = jnp.asarray

    def _rec_inputs():
        import jax
        import jax.numpy as jnp
        _rk = jax.random.key(seed)
        x = -0.0002928 + 1 * jax.random.normal(jax.random.fold_in(_rk, 1), (8, 512, 256), jnp.float32)
        _lenS = 512 - jax.random.randint(jax.random.fold_in(_rk, 7), (8,), 0, max(1, 512 // 4) + 1, jnp.int32)
        _lenS2 = 512 - jax.random.randint(jax.random.fold_in(_rk, 8), (8,), 0, max(1, 512 // 4) + 1, jnp.int32)
        _ctx_1024P = jax.random.normal(jax.random.fold_in(_rk, 11), (8, 16, 256), jnp.float32)
        _ctx_1024c = jax.random.dirichlet(jax.random.fold_in(_rk, 511), 0.3 * jnp.ones((16,), jnp.float32), (8, 512))
        _ctx_1024t = jnp.einsum('bsk,bkd->bsd', _ctx_1024c, _ctx_1024P)
        _ctx_1024t = _ctx_1024t * jax.lax.rsqrt(jnp.mean(jnp.square(_ctx_1024t)) + 1e-12) * 0.953939
        ctx_1024 = -1.39393e-06 + 0.999914 * (_ctx_1024t + 0.3 * jax.random.normal(jax.random.fold_in(_rk, 611), (8, 512, 256), jnp.float32))
        return (x, ctx_1024)
    x, ctx_1024 = _rec_inputs()

    def _L0_xattn_setup():
        import jax, jax.numpy as jnp
        import numpy as np
        EPS_BACKEND = 1e-06
        NORM_EPS = 1e-06
        NUM_HEADS = 4

        def _mlstm_forward(q, k, v, ig_kernel, ig_bias, fg_kernel, fg_bias, outnorm_weight):
            B, S, E = q.shape
            NH = ig_bias.shape[0]
            DH = E // NH
            gate_input = jnp.concatenate([q, k, v], axis=-1)
            igate = gate_input @ ig_kernel + ig_bias
            fgate = gate_input @ fg_kernel + fg_bias
            qh = q.reshape(B, S, NH, DH).transpose(0, 2, 1, 3)
            kh = k.reshape(B, S, NH, DH).transpose(0, 2, 1, 3)
            vh = v.reshape(B, S, NH, DH).transpose(0, 2, 1, 3)
            ig = igate.transpose(0, 2, 1)
            fg = fgate.transpose(0, 2, 1)
            log_fg = jax.nn.log_sigmoid(fg)
            cums = jnp.concatenate([jnp.zeros((B, NH, 1), log_fg.dtype), jnp.cumsum(log_fg, axis=-1)], axis=-1)
            fg_mat = cums[..., :, None] - cums[..., None, :]
            mask = jnp.tril(jnp.ones((S + 1, S + 1), bool))
            fg_mat = jnp.where(mask, fg_mat, -jnp.inf)[..., 1:, 1:]
            log_D = fg_mat + ig[..., None, :]
            max_log_D = jnp.max(log_D, axis=-1, keepdims=True)
            D = jnp.exp(log_D - max_log_D)
            qk = jnp.einsum('bnsd,bntd->bnst', qh, kh) / jnp.sqrt(jnp.float32(DH))
            C = qk * D
            normalizer = jnp.maximum(jnp.abs(C.sum(-1, keepdims=True)), jnp.exp(-max_log_D))
            h = jnp.einsum('bnst,bntd->bnsd', C / (normalizer + EPS_BACKEND), vh)
            h = h.transpose(0, 2, 1, 3)
            mean = h.mean(-1, keepdims=True)
            var = h.var(-1, keepdims=True)
            hn = (h - mean) * jax.lax.rsqrt(var + NORM_EPS) * outnorm_weight
            return hn.reshape(B, S, E)
        key = jax.random.key(seed)
        ks = jax.random.split(key, 8)
        B, S, E, NH = (2, 512, 256, NUM_HEADS)
        DH = E // NH
        q = jax.random.normal(ks[0], (B, S, E), jnp.float32)
        k = jax.random.normal(ks[1], (B, S, E), jnp.float32)
        v = jax.random.normal(ks[2], (B, S, E), jnp.float32)
        ig_kernel = jax.random.normal(ks[3], (3 * E, NH), jnp.float32) * 0.02
        fg_kernel = jax.random.normal(ks[4], (3 * E, NH), jnp.float32) * 0.02
        ig_bias = jax.random.normal(ks[5], (NH,), jnp.float32) * 0.1
        fg_bias = jnp.linspace(3.0, 6.0, NH, dtype=jnp.float32)
        outnorm_weight = jnp.ones((NH, DH), jnp.float32)
        return {'q': q, 'k': k, 'v': v, 'ig_kernel': ig_kernel, 'ig_bias': ig_bias, 'fg_kernel': fg_kernel, 'fg_bias': fg_bias, 'outnorm_weight': outnorm_weight}
    _L0_xattn_all = _L0_xattn_setup()
    _L0_xattn_in = {k: v for k, v in _L0_xattn_all.items() if k in ('ig_kernel', 'ig_bias', 'fg_kernel', 'fg_bias', 'outnorm_weight')}
    del _L0_xattn_all

    def _L0_ffn_setup():
        import jax, jax.numpy as jnp
        import numpy as np
        B, S, D, H, M, E, K = (4, 256, 256, 16, 2, 8, 2)
        KD = D // H
        F = 2 * D
        EPS = 1e-06

        def _ln(x, g, b):
            m = jnp.mean(x, axis=-1, keepdims=True)
            v = jnp.mean(jnp.square(x - m), axis=-1, keepdims=True)
            return (x - m) * jax.lax.rsqrt(v + EPS) * g + b
        key = jax.random.key(seed)
        ks = jax.random.split(key, 12)
        r = lambda i, shape: jax.random.normal(ks[i], shape, jnp.float32) * 0.02
        return {'x': jax.random.normal(ks[0], (B, S, D), jnp.float32), 'ln1_g': jnp.ones((D,), jnp.float32), 'ln1_b': jnp.zeros((D,), jnp.float32), 'ln2_g': jnp.ones((D,), jnp.float32), 'ln2_b': jnp.zeros((D,), jnp.float32), 'mha_wq': r(1, (M, D, H, KD)), 'mha_bq': jnp.zeros((M, H, KD), jnp.float32), 'mha_wk': r(2, (M, D, H, KD)), 'mha_bk': jnp.zeros((M, H, KD), jnp.float32), 'mha_wv': r(3, (M, D, H, KD)), 'mha_bv': jnp.zeros((M, H, KD), jnp.float32), 'mha_wo': r(4, (M, H, KD, D)), 'mha_bo': jnp.zeros((M, D), jnp.float32), 'mha_rw': r(5, (D, M)), 'mha_rb': jnp.zeros((M,), jnp.float32), 'ffn_rw': r(6, (D, E)), 'ffn_rb': jnp.zeros((E,), jnp.float32), 'fw1': r(7, (E, D, F)), 'fw2': r(8, (E, F, D))}
    _L0_ffn_all = _L0_ffn_setup()
    _L0_ffn_in = {k: v for k, v in _L0_ffn_all.items() if k in ('ln1_g', 'ln1_b', 'ln2_g', 'ln2_b', 'mha_wq', 'mha_bq', 'mha_wk', 'mha_bk', 'mha_wv', 'mha_bv', 'mha_wo', 'mha_bo', 'mha_rw', 'mha_rb', 'ffn_rw', 'ffn_rb', 'fw1', 'fw2')}
    del _L0_ffn_all
    return {'x': x, 'ctx_1024': ctx_1024, 'L0_xattn_ig_kernel': _L0_xattn_in['ig_kernel'], 'L0_xattn_ig_bias': _L0_xattn_in['ig_bias'], 'L0_xattn_fg_kernel': _L0_xattn_in['fg_kernel'], 'L0_xattn_fg_bias': _L0_xattn_in['fg_bias'], 'L0_xattn_outnorm_weight': _L0_xattn_in['outnorm_weight'], 'L0_ffn_ln1_g': _L0_ffn_in['ln1_g'], 'L0_ffn_ln1_b': _L0_ffn_in['ln1_b'], 'L0_ffn_ln2_g': _L0_ffn_in['ln2_g'], 'L0_ffn_ln2_b': _L0_ffn_in['ln2_b'], 'L0_ffn_mha_wq': _L0_ffn_in['mha_wq'], 'L0_ffn_mha_bq': _L0_ffn_in['mha_bq'], 'L0_ffn_mha_wk': _L0_ffn_in['mha_wk'], 'L0_ffn_mha_bk': _L0_ffn_in['mha_bk'], 'L0_ffn_mha_wv': _L0_ffn_in['mha_wv'], 'L0_ffn_mha_bv': _L0_ffn_in['mha_bv'], 'L0_ffn_mha_wo': _L0_ffn_in['mha_wo'], 'L0_ffn_mha_bo': _L0_ffn_in['mha_bo'], 'L0_ffn_mha_rw': _L0_ffn_in['mha_rw'], 'L0_ffn_mha_rb': _L0_ffn_in['mha_rb'], 'L0_ffn_ffn_rw': _L0_ffn_in['ffn_rw'], 'L0_ffn_ffn_rb': _L0_ffn_in['ffn_rb'], 'L0_ffn_fw1': _L0_ffn_in['fw1'], 'L0_ffn_fw2': _L0_ffn_in['fw2']}

def reference(x, ctx_1024, L0_xattn_ig_kernel, L0_xattn_ig_bias, L0_xattn_fg_kernel, L0_xattn_fg_bias, L0_xattn_outnorm_weight, L0_ffn_ln1_g, L0_ffn_ln1_b, L0_ffn_ln2_g, L0_ffn_ln2_b, L0_ffn_mha_wq, L0_ffn_mha_bq, L0_ffn_mha_wk, L0_ffn_mha_bk, L0_ffn_mha_wv, L0_ffn_mha_bv, L0_ffn_mha_wo, L0_ffn_mha_bo, L0_ffn_mha_rw, L0_ffn_mha_rb, L0_ffn_ffn_rw, L0_ffn_ffn_rb, L0_ffn_fw1, L0_ffn_fw2):
    import jax
    import jax.numpy as jnp

    def _L0_xattn_ref(q, k, v, ig_kernel, ig_bias, fg_kernel, fg_bias, outnorm_weight):
        import jax, jax.numpy as jnp
        import numpy as np
        EPS_BACKEND = 1e-06
        NORM_EPS = 1e-06
        NUM_HEADS = 4

        def _mlstm_forward(q, k, v, ig_kernel, ig_bias, fg_kernel, fg_bias, outnorm_weight):
            B, S, E = q.shape
            NH = ig_bias.shape[0]
            DH = E // NH
            gate_input = jnp.concatenate([q, k, v], axis=-1)
            igate = gate_input @ ig_kernel + ig_bias
            fgate = gate_input @ fg_kernel + fg_bias
            qh = q.reshape(B, S, NH, DH).transpose(0, 2, 1, 3)
            kh = k.reshape(B, S, NH, DH).transpose(0, 2, 1, 3)
            vh = v.reshape(B, S, NH, DH).transpose(0, 2, 1, 3)
            ig = igate.transpose(0, 2, 1)
            fg = fgate.transpose(0, 2, 1)
            log_fg = jax.nn.log_sigmoid(fg)
            cums = jnp.concatenate([jnp.zeros((B, NH, 1), log_fg.dtype), jnp.cumsum(log_fg, axis=-1)], axis=-1)
            fg_mat = cums[..., :, None] - cums[..., None, :]
            mask = jnp.tril(jnp.ones((S + 1, S + 1), bool))
            fg_mat = jnp.where(mask, fg_mat, -jnp.inf)[..., 1:, 1:]
            log_D = fg_mat + ig[..., None, :]
            max_log_D = jnp.max(log_D, axis=-1, keepdims=True)
            D = jnp.exp(log_D - max_log_D)
            qk = jnp.einsum('bnsd,bntd->bnst', qh, kh) / jnp.sqrt(jnp.float32(DH))
            C = qk * D
            normalizer = jnp.maximum(jnp.abs(C.sum(-1, keepdims=True)), jnp.exp(-max_log_D))
            h = jnp.einsum('bnst,bntd->bnsd', C / (normalizer + EPS_BACKEND), vh)
            h = h.transpose(0, 2, 1, 3)
            mean = h.mean(-1, keepdims=True)
            var = h.var(-1, keepdims=True)
            hn = (h - mean) * jax.lax.rsqrt(var + NORM_EPS) * outnorm_weight
            return hn.reshape(B, S, E)
        return _mlstm_forward(q, k, v, ig_kernel, ig_bias, fg_kernel, fg_bias, outnorm_weight)

    def _L0_ffn_ref(x, ln1_g, ln1_b, ln2_g, ln2_b, mha_wq, mha_bq, mha_wk, mha_bk, mha_wv, mha_bv, mha_wo, mha_bo, mha_rw, mha_rb, ffn_rw, ffn_rb, fw1, fw2):
        import jax, jax.numpy as jnp
        import numpy as np
        B, S, D, H, M, E, K = (4, 256, 256, 16, 2, 8, 2)
        KD = D // H
        F = 2 * D
        EPS = 1e-06

        def _ln(x, g, b):
            m = jnp.mean(x, axis=-1, keepdims=True)
            v = jnp.mean(jnp.square(x - m), axis=-1, keepdims=True)
            return (x - m) * jax.lax.rsqrt(v + EPS) * g + b
        n1 = _ln(x, ln1_g, ln1_b)
        mha_probs = jax.nn.softmax(jnp.mean(n1, axis=1) @ mha_rw + mha_rb, axis=-1)
        q = jnp.einsum('btd,mdhk->mbhtk', n1, mha_wq) + mha_bq[:, None, :, None, :]
        kk = jnp.einsum('btd,mdhk->mbhtk', n1, mha_wk) + mha_bk[:, None, :, None, :]
        v = jnp.einsum('btd,mdhk->mbhtk', n1, mha_wv) + mha_bv[:, None, :, None, :]
        scores = jnp.einsum('mbhtk,mbhsk->mbhts', q, kk) / jnp.sqrt(jnp.float32(KD))
        attn = jax.nn.softmax(scores, axis=-1)
        ctx = jnp.einsum('mbhts,mbhsk->mbthk', attn, v)
        mha_out = jnp.einsum('mbthk,mhkd->mbtd', ctx, mha_wo) + mha_bo[:, None, None, :]
        x = x + jnp.einsum('mbtd,bm->btd', mha_out, mha_probs)
        n2 = _ln(x, ln2_g, ln2_b)
        ffn_probs = jax.nn.softmax(jnp.mean(n2, axis=1) @ ffn_rw + ffn_rb, axis=-1)
        topk_p, topk_i = jax.lax.top_k(ffn_probs, K)
        topk_p = topk_p / jnp.sum(topk_p, axis=-1, keepdims=True)
        sw1 = fw1[topk_i]
        sw2 = fw2[topk_i]
        h = jax.nn.gelu(jnp.einsum('btd,bkdf->bktf', n2, sw1), approximate=False)
        eo = jnp.einsum('bktf,bkfd->bktd', h, sw2)
        return x + jnp.einsum('bktd,bk->btd', eo, topk_p)
    x = x + _L0_xattn_ref(_layernorm(x, axis=-1), ctx_1024, ctx_1024, L0_xattn_ig_kernel, L0_xattn_ig_bias, L0_xattn_fg_kernel, L0_xattn_fg_bias, L0_xattn_outnorm_weight)
    x = x + _L0_ffn_ref(_layernorm(x, axis=-1), L0_ffn_ln1_g, L0_ffn_ln1_b, L0_ffn_ln2_g, L0_ffn_ln2_b, L0_ffn_mha_wq, L0_ffn_mha_bq, L0_ffn_mha_wk, L0_ffn_mha_bk, L0_ffn_mha_wv, L0_ffn_mha_bv, L0_ffn_mha_wo, L0_ffn_mha_bo, L0_ffn_mha_rw, L0_ffn_mha_rb, L0_ffn_ffn_rw, L0_ffn_ffn_rb, L0_ffn_fw1, L0_ffn_fw2)
    return x

_drawn_inputs = setup_inputs


def setup_inputs(seed=0):
    import zlib

    import numpy as np

    out = dict(_drawn_inputs(seed))
    spreads = {'L0_xattn_outnorm_weight': (1.0, 0.2),
     'L0_ffn_ln1_g': (1.0, 0.6),
     'L0_ffn_ln1_b': (0.0, 0.739),
     'L0_ffn_ln2_g': (1.0, 0.6),
     'L0_ffn_ln2_b': (0.0, 1.674),
     'L0_ffn_mha_bq': (0.0, 0.8),
     'L0_ffn_mha_bk': (0.0, 2.0),
     'L0_ffn_mha_bv': (0.0, 0.591),
     'L0_ffn_mha_bo': (0.0, 0.525),
     'L0_ffn_mha_rb': (0.0, 2.0),
     'L0_ffn_ffn_rb': (0.0, 0.763)}
    factors = {'L0_xattn_ig_bias': 64.0,
     'L0_ffn_mha_wq': 8.0,
     'L0_ffn_mha_wk': 8.0,
     'L0_ffn_mha_wv': 8.0,
     'L0_ffn_mha_wo': 4.731,
     'L0_ffn_mha_rw': 8.0,
     'L0_ffn_ffn_rw': 4.834,
     'L0_ffn_fw1': 2.711}
    for name, (base, spread) in spreads.items():
        noise = np.random.default_rng([zlib.crc32(name.encode()), seed]).standard_normal(out[name].shape)
        drawn = base * np.exp(spread * noise) if base else spread * noise
        out[name] = jnp.asarray(drawn.astype(out[name].dtype))
    for name, factor in factors.items():
        out[name] = (out[name] * factor).astype(out[name].dtype)
    return out
```

```python
from contextlib import ExitStack

import numpy as np
import concourse.bass as bass
from concourse import mybir

F32 = mybir.dt.float32
BF16 = mybir.dt.bfloat16
U32 = mybir.dt.uint32
ALU = mybir.AluOpType
ACT = mybir.ActivationFunctionType
AX = mybir.AxisListType.X

P = 128
ENGINES = ("pe", "act", "dve", "pool", "sp")


class Point:

    def __init__(self, sem_name, region, count, unit):
        self.sem_name, self.region, self.count, self.unit = sem_name, region, count, unit


class Queues:

    def __init__(self):
        self.items = {e: {} for e in ENGINES}
        self.counts = {}
        self.region = None

    def enter(self, region):
        self.region = region

    def _point(self, sem_name, unit):
        key = (sem_name, self.region)
        self.counts[key] = self.counts.get(key, 0) + unit
        return Point(sem_name, self.region, self.counts[key], unit)

    def put(self, engine, fn, *waits):
        point = self._point(engine, 1)
        self.items[engine].setdefault(self.region, []).append((fn, [w for w in waits if w is not None], point))
        return point

    def dma(self, engine, stream, fn, *waits):
        point = self._point(stream, 16)
        self.items[engine].setdefault(self.region, []).append((fn, [w for w in waits if w is not None], point))
        return point

    def total(self, sem_name, region):
        return self.counts.get((sem_name, region), 0)


class Banks:

    def __init__(self, banks):
        self.banks, self.busy, self.at = banks, {b: () for b in banks}, 0

    def take(self, n=1):
        got = [self.banks[(self.at + i) % len(self.banks)] for i in range(n)]
        self.at += n
        waits = [w for b in got for w in self.busy[b]]
        return (got if n > 1 else got[0]), waits

    def free(self, bank, *points):
        self.busy[bank] = points


def build(nc, d, out):
    B, S, E = d["x"].shape
    NT = S // P
    KC = E // P
    NH = d["ig_bias"].shape[0]
    DH = E // NH
    NG = NH * NT
    M, _, H, KD = d["wq"].shape
    HC = P // KD
    NX = d["ffn_rb"].shape[0]
    FF = d["fw1"].shape[2]
    FC = FF // P
    TOPK = 2
    QUAD = 4
    NQ = M * H // QUAD
    TERMS_K = (0, 0, 1, 1, 0, 2)
    TERMS_Q = (0, 1, 0, 1, 2, 0)
    KROWS = len(TERMS_K) * KD
    VW = 32

    q = Queues()
    ctx = ExitStack()
    with ctx:
        def sb(name, shape, dt=F32):
            return ctx.enter_context(nc.sbuf_tensor(name, shape, dt))

        psum = ctx.enter_context(nc.psum_tensor("psum", [P, 8, 512], F32))

        ident = sb("ident", [P, P])
        onesrow = sb("onesrow", [NH, S])
        onecol = sb("onecol", [P, 1])
        neghalf = sb("neghalf", [P, NG])
        headsel = sb("headsel", [NH, NH, P])
        wgate = sb("wgate", [P, 3 * KC, 2, NH])
        wgkv = sb("wgkv", [P, KC, 2, NH])
        gbias = sb("gbias", [NH, 2])
        onw = sb("onw", [P, E])
        ln1 = sb("ln1", [P, 2, KC])
        ln2 = sb("ln2", [P, 2, KC])
        wq = sb("wq", [P, KC, M, H * KD])
        wk = sb("wk", [P, KC, M, H * KD])
        wv = sb("wv", [P, KC, M, H * KD])
        bq = sb("bq", [P, M, KC])
        bqs = sb("bqs", [P, M, KC])
        bk = sb("bk", [P, M, KC])
        bv = sb("bv", [P, M, H * KD])
        wo = sb("wo", [P, M, KC, E])
        bo = sb("bo", [P, M, E])
        rw = sb("rw", [P, KC, M])
        rb = sb("rb", [P, M])
        fr = sb("fr", [P, KC, NX])
        fb = sb("fb", [P, NX])

        xin = sb("xin", [P, NT, E])
        kin = sb("kin", [P, NT, E])
        vaug = sb("vaug", [P, NT, NH, DH + 1])
        vdec = sb("vdec", [P, NT - 1, NH, DH + 1])
        stats = sb("stats", [P, NT, 6])
        mv = sb("mv", [P, NT, 2])
        rstd = sb("rstd", [P, 4, NT])
        qn = sb("qn", [P, NT, E])
        qT = sb("qT", [P, KC, S])
        kT = sb("kT", [P, KC, S])
        proj = sb("proj", [P, 2, S])
        resid = sb("resid", [P, 2, S])
        gi, gf = proj[0:NH, 0], proj[0:NH, 1]
        ga, lf = resid[0:NH, 0], resid[0:NH, 1]
        cx = sb("cx", [P, NT, M, H * KD])
        hh = cx[:, 0:2].rearrange("p a m (g d) -> p (a m g) d", d=DH)
        hs = cx[:, 2:4].rearrange("p a m (g d) -> p (a m g) d", d=DH)
        rows = sb("rows", [NH, 3, S])
        cols = sb("cols", [P, 3, NT, NH])
        gend = sb("gend", [P, NH, NT])
        dec = sb("dec", [P, 4, NT, NH])
        prob = sb("prob", [P, 2, QUAD, S])
        dmat, cmat = prob[:, 0], prob[:, 1]
        state = sb("state", [P, NT - 1, NH // 2, DH + 1])
        num = sb("num", [P, NT, NH, DH + 1])
        inter = sb("inter", [P, NH, DH + 1])
        nrm = sb("nrm", [P, 2, NG])
        hm = sb("hm", [P, 4, NG])
        x2 = sb("x2", [P, NT, E])
        xf = sb("xf", [P, NT, E])
        n1 = sb("n1", [P, NT, E])
        n1T = sb("n1T", [P, KC, S])
        msum = sb("msum", [P, KC])
        mbc = sb("mbc", [P, KC, P])
        mp = sb("mp", [P, M])
        sm1 = sb("sm1", [P, 4])
        parts = sb("parts", [P, 2, 3, S], BF16)
        kst = sb("kst", [P, M * H, S], BF16)
        qst = sb("qst", [P, M * H, S], BF16)
        vst = sb("vst", [P, NT, M * H, VW])
        mx = sb("mx", [P, M * H, NT])
        mrow = sb("mrow", [QUAD * NT, 2, 2, P], BF16)
        rden = sb("rden", [P, 2, NT, QUAD])
        ep = sb("ep", [P, NX])
        top = sb("top", [P, NX])
        topi = sb("topi", [P, NX], U32)
        gate = sb("gate", [P, TOPK])
        es = sb("es", [P, 4])
        n2, n2T, acc, x3 = n1, n1T, xf, qn
        ctxs = kin[:].rearrange("p (i a) n -> p i (a n)", i=2)
        hT = prob[:, 0]
        cxT = prob[:, 1].rearrange("p (m c) s -> p m c s", m=M)
        words = TOPK * KC * FF * 2 // S
        w1 = qst[:, 0:words, :].rearrange("p h s -> p (h s)").bitcast(F32).rearrange("p (k c f) -> p k c f", k=TOPK, c=KC)
        w2 = qst[:, words:2 * words, :].rearrange("p h s -> p (h s)").bitcast(F32).rearrange(
            "p (k c n) -> p k c n", k=TOPK, c=FC)

        parts_dram = nc.dram_tensor("parts_dram", (2, M, KC, 3, P, S), BF16, kind="Internal").ap()

        def sem(name):
            return ctx.enter_context(nc.semaphore(name))

        def bank(i, n=1):
            return psum[:, i:i + n, :]

        q.enter("setup")

        def load(stream, dst, src):
            return q.dma("sp", stream, lambda e, b: e.dma_start(dst, src, allow_slow_non_contiguous=True))

        for g, name in enumerate(("ig_kernel", "fg_kernel")):
            load("weights", wgate[:, :, g, :], d[name].rearrange("(c p) h -> p c h", p=P))
            load("weights", gbias[:, g:g + 1], d[("ig_bias", "fg_bias")[g]].rearrange("(h o) -> h o", o=1))
        load("weights", onw[:], d["outnorm_weight"].rearrange("(o h) d -> o (h d)", o=1).to_broadcast([P, E]))
        for i, t in enumerate((ln1, ln2)):
            for j, s in enumerate("gb"):
                load("weights", t[:, j, :], d[f"ln{i + 1}_{s}"].rearrange("(c p) -> p c", p=P))
        for t, name in ((wq, "wq"), (wk, "wk"), (wv, "wv")):
            for m in range(M):
                load("weights", t[:, :, m, :], d[name][m].rearrange("(c p) h k -> p c (h k)", p=P))
        for t, name in ((bq, "bq"), (bk, "bk")):
            for m in range(M):
                load("weights", t[:, m, :], d[name][m].rearrange("(c h) k -> (h k) c", c=KC))
        load("weights", bv[:], d["bv"].rearrange("(o m) h k -> o m (h k)", o=1).to_broadcast([P, M, H * KD]))
        for m in range(M):
            load("weights", wo[:, m, :, :], d["wo"][m].rearrange("(c h) k n -> (h k) c n", c=KC))
        load("weights", bo[:], d["bo"].rearrange("(o m) n -> o m n", o=1).to_broadcast([P, M, E]))
        load("weights", rw[:], d["rw"].rearrange("(c p) m -> p c m", p=P))
        load("weights", rb[:], d["rb"].rearrange("(o m) -> o m", o=1).to_broadcast([P, M]))
        load("weights", fr[:], d["ffn_rw"].rearrange("(c p) m -> p c m", p=P))
        weights = load("weights", fb[:], d["ffn_rb"].rearrange("(o m) -> o m", o=1).to_broadcast([P, NX]))

        zero = q.put("pool", lambda e, b: e.memset(ident[:], 0.0))
        q.put("pool", lambda e, b: e.affine_select(out=ident[:], in_=ident[:], compare_op=ALU.not_equal, fill=1.0,
                                                   base=0, pattern=[[-1, P]], channel_multiplier=1), zero)
        q.put("pool", lambda e, b: e.memset(onesrow[:], 1.0))
        q.put("pool", lambda e, b: e.memset(onecol[:], 1.0))
        q.put("pool", lambda e, b: e.memset(neghalf[:], -0.5))
        q.put("pool", lambda e, b: e.memset(vaug[:, :, :, DH:DH + 1], 1.0))
        q.put("pool", lambda e, b: e.memset(vst[:, :, :, KD:KD + 1], 1.0))
        consts = q.put("pool", lambda e, b: e.memset(vst[:, :, :, KD + 1:VW], 0.0))
        q.put("dve", lambda e, b: e.memset(kst[KROWS:KROWS + 2, :, :], 1.0))
        for h in range(NH):
            q.put("dve", lambda e, b, h=h: e.tensor_copy(headsel[:, h, :], ident[0:NH, h:h + 1].to_broadcast([NH, P])),
                  consts)
        q.put("dve", lambda e, b: e.tensor_tensor(wgkv[:], wgate[:, KC:2 * KC], wgate[:, 2 * KC:3 * KC], ALU.add),
              weights)
        ready = q.put("dve", lambda e, b: e.tensor_scalar(bqs[:], bq[:], KD ** -0.5, None, ALU.mult), weights)

        q.enter("batch")
        ring = Banks(list(range(8)))

        def mm(out_, lhsT, rhs, start, stop, *waits, **kw):
            return q.put("pe", lambda e, b: e.matmul(out_, lhsT, rhs, start=start, stop=stop, **kw), *waits)

        def tr(out_, in_, n, *waits):
            return q.put("pe", lambda e, b: e.transpose(out_, in_, ident[0:n, 0:n]), *waits)

        def act(out_, in_, f, *waits, **kw):
            return q.put("act", lambda e, b: e.activation(out_, in_, f, **kw), *waits)

        def tt(eng, out_, a, c, op, *waits):
            return q.put(eng, lambda e, b: e.tensor_tensor(out_, a, c, op), *waits)

        def ts(eng, out_, a, s1, s2, op0, op1, *waits):
            if op1 is None:
                return q.put(eng, lambda e, b: e.tensor_scalar(out_, a, s1, None, op0), *waits)
            return q.put(eng, lambda e, b: e.tensor_scalar(out_, a, s1, s2, op0, op1), *waits)

        def stt(out_, a, s, c, op0, op1, *waits):
            return q.put("dve", lambda e, b: e.scalar_tensor_tensor(out=out_, in0=a, scalar=s, in1=c,
                                                                    op0=op0, op1=op1), *waits)

        def red(out_, in_, op, *waits):
            return q.put("dve", lambda e, b: e.tensor_reduce(out_, in_, AX, op), *waits)

        def copy(eng, out_, in_, *waits):
            return q.put(eng, lambda e, b: e.tensor_copy(out_, in_), *waits)

        def power(out_, in_, n, *waits):
            return q.put("pool", lambda e, b: e.tensor_tensor(out_, in_, neghalf[:, 0:n], ALU.pow), *waits)

        def moments(src, *waits):
            for t in range(NT):
                a = q.put("dve", lambda e, b, t=t: e.bn_stats(stats[:, t, :], src[:, t, :]), *waits)
                last = q.put("dve", lambda e, b, t=t: e.bn_aggr(mv[:, t, :], stats[:, t, :]), a)
            return last

        def rows_to_columns(src, evacuate, *waits):
            done = []
            for c in range(KC):
                bk_, free = ring.take()
                for t in range(NT):
                    last = tr(psum[:, bk_, t * P:(t + 1) * P], src[:, t, c * P:(c + 1) * P], P, *waits, *free)
                done.append(evacuate(c, psum[:, bk_, :], last))
                ring.free(bk_, done[-1])
            return done

        ldx = q.dma("sp", "load_x", lambda e, b: e.dma_start(
            xin[:], d["x"][bass.ds(b, 1)].rearrange("o (t p) n -> p (o t) n", p=P)))
        ldk = q.dma("sp", "load_ctx", lambda e, b: e.dma_start(
            kin[:], d["ctx_1024"][bass.ds(b, 1)].rearrange("o (t p) n -> p (o t) n", p=P)))

        mo = moments(xin, ldx)
        e1 = ts("dve", rstd[:, 0, :], mv[:, :, 1], 1e-5, None, ALU.add, None, mo)
        pw = power(rstd[:, 1, :], rstd[:, 0, :], NT, e1)
        for t in range(NT):
            qdone = ts("dve", qn[:, t, :], xin[:, t, :], mv[:, t, 0:1], rstd[:, 1, t:t + 1], ALU.subtract, ALU.mult, pw)
        vcopy = copy("pool", vaug[:, :, :, 0:DH], kin[:].rearrange("p t (h d) -> p t h d", h=NH), ldk)
        qTd = rows_to_columns(qn, lambda c, ps, w: act(qT[:, c, :], ps, ACT.Copy, w), qdone)
        kTd = rows_to_columns(kin, lambda c, ps, w: copy("dve", kT[:, c, :], ps, w), ldk)

        def gate_rows(g):
            bk_, free = ring.take()
            for c in range(KC):
                mm(psum[0:NH, bk_, :], wgate[:, c, g, :], qT[:, c, :], c == 0, False, *qTd, *free)
            for c in range(KC):
                last = mm(psum[0:NH, bk_, :], wgkv[:, c, g, :], kT[:, c, :], False, c == KC - 1, *kTd)
            return bk_, last

        bi, wi = gate_rows(0)
        bf, wf = gate_rows(1)
        igd = act(gi, psum[0:NH, bi, :], ACT.Identity, wi, bias=gbias[:, 0:1])
        fgd = act(gf, psum[0:NH, bf, :], ACT.Identity, wf, bias=gbias[:, 1:2])
        ring.free(bi, igd)
        ring.free(bf, fgd)
        a1 = act(ga, gf, ACT.Abs, fgd)
        a2 = act(ga, ga, ACT.Exp, a1, scale=-1.0)
        a3 = act(ga, ga, ACT.Ln, a2, bias=onecol[0:NH, :])
        lfd = stt(lf, gf, 0.0, ga, ALU.min, ALU.subtract, a3)
        Fd = q.put("dve", lambda e, b: e.tensor_tensor_scan(gf, onesrow[:], lf, 0.0, ALU.mult, ALU.add), lfd)
        gd = tt("dve", rows[:, 0, :], gi, gf, ALU.subtract, Fd, igd)
        Gd = q.put("dve", lambda e, b: e.tensor_tensor_scan(rows[:, 1, :], rows[:, 0, :], rows[:, 0, :], -3.0e38,
                                                            ALU.max, ALU.max), gd)
        Md = tt("dve", rows[:, 2, :], gf, rows[:, 1, :], ALU.add, Gd)

        bc, free = ring.take()
        for r in range(3):
            for c in range(NT):
                o = (r * NT + c) * NH
                last = tr(psum[:, bc, o:o + NH], rows[:, r, c * P:(c + 1) * P], NH, Md, *free)
        cold = copy("dve", cols[:].rearrange("p r c h -> p (r c h)"), psum[:, bc, 0:3 * NG], last)
        ring.free(bc, cold)
        dexp = []
        gends = []
        for h in range(NH):
            bg, free = ring.take()
            w = mm(psum[:, bg, :], headsel[:, h, :], rows[:, 1, :], True, True, Md, *free)
            gends.append(copy("dve", gend[:, h, :], psum[:, bg, P - 1::P], w))
            for c in range(NT):
                last = act(dmat[:, h, c * P:(c + 1) * P], psum[:, bg, c * P:(c + 1) * P], ACT.Exp, w, cold, gends[-1],
                           bias=cols[:, 0, c, h:h + 1], scale=-1.0)
            ring.free(bg, last)
            dexp.append(last)
        masked = []
        for h in range(NH):
            masked.append(q.put("pool", lambda e, b, h=h: e.affine_select(
                out=dmat[:, h, :].rearrange("p (c s) -> p c s", c=NT), in_=dmat[:, h, :].rearrange("p (c s) -> p c s", c=NT),
                compare_op=ALU.is_ge, fill=0.0, base=0, pattern=[[0, NT], [1, P]], channel_multiplier=-1), dexp[h]))

        ge = gend[:].rearrange("p h c -> p c h")
        tt("dve", dec[:, 0, 1:NT, :], ge[:, 0:NT - 1, :], cols[:, 1, 1:NT, :], ALU.subtract, *gends, cold)
        tt("dve", dec[:, 1, 0:NT - 1, :], cols[:, 0, 0:NT - 1, :], ge[:, 0:NT - 1, :], ALU.subtract)
        tt("dve", dec[:, 2, 1:NT - 1, :], ge[:, 0:NT - 2, :], ge[:, 1:NT - 1, :], ALU.subtract)
        dd = ts("dve", dec[:, 3, :, :], cols[:, 2, :, :], -1.0, None, ALU.mult, None)
        act(dec[:, 0, 1:NT, :], dec[:, 0, 1:NT, :], ACT.Exp, dd)
        act(dec[:, 1, 0:NT - 1, :], dec[:, 1, 0:NT - 1, :], ACT.Exp)
        act(dec[:, 2, 1:NT - 1, :], dec[:, 2, 1:NT - 1, :], ACT.Exp)
        decd = act(dec[:, 3, :, :], dec[:, 3, :, :], ACT.Exp)
        wsc = ts("dve", dec[:, 1, 0:NT - 1, :], dec[:, 1, 0:NT - 1, :], DH ** -0.5, None, ALU.mult, None, decd)
        vw = tt("pool", vdec[:], vaug[:, 0:NT - 1],
                dec[:, 1, 0:NT - 1, :].unsqueeze(3).to_broadcast([P, NT - 1, NH, DH + 1]), ALU.mult, wsc, vcopy)

        cd = []
        for h in range(NH):
            ba, free = ring.take()
            o = DH * (h % 2)
            for c in range(NT):
                s = slice(c * P, (c + 1) * P)
                last = mm(psum[:, ba, s], kT[o:o + DH, h // 2, s], qT[o:o + DH, h // 2, s], True, True,
                          *qTd, *kTd, *free)
            cd.append(stt(cmat[:, h, :], psum[:, ba, :], DH ** -0.5, dmat[:, h, :], ALU.mult, ALU.mult, last, masked[h]))
            ring.free(ba, cd[-1])

        st = None
        for c in range(NT - 1):
            bs, free = ring.take()
            for h in range(NH):
                o = DH * (h % 2)
                last = mm(psum[o:o + DH, bs, (h // 2) * (DH + 1):(h // 2 + 1) * (DH + 1)],
                          kin[:, c, h * DH:(h + 1) * DH], vdec[:, c, h, :], True, True, vw, *free)
            if c == 0:
                st = copy("dve", state[:, 0, :, :].rearrange("p a n -> p (a n)"),
                          psum[:, bs, 0:(NH // 2) * (DH + 1)], last)
            else:
                prev = st
                for h in range(NH):
                    o = DH * (h % 2)
                    st = stt(state[o:o + DH, c, h // 2, :], state[o:o + DH, c - 1, h // 2, :],
                             dec[o:o + DH, 2, c, h:h + 1],
                             psum[o:o + DH, bs, (h // 2) * (DH + 1):(h // 2 + 1) * (DH + 1)],
                             ALU.mult, ALU.add, last, prev, decd)
            ring.free(bs, st)

        numd = []
        for c in range(NT):
            s = slice(c * P, (c + 1) * P)
            bn, free = ring.take()
            for h in range(NH):
                wi_ = mm(psum[:, bn, h * (DH + 1):(h + 1) * (DH + 1)], cmat[:, h, s], vaug[:, c, h, :], True, True,
                         *cd, vcopy, *free)
            intra = psum[:, bn, 0:NH * (DH + 1)].rearrange("p (h n) -> p h n", h=NH)
            if c == 0:
                numd.append(copy("dve", num[:, c], intra, wi_))
            else:
                t1 = []
                for par in range(2):
                    bx, free = ring.take()
                    o = DH * par
                    for hp in range(NH // 2):
                        wx = mm(psum[:, bx, hp * (DH + 1):(hp + 1) * (DH + 1)], qT[o:o + DH, hp, s],
                                state[o:o + DH, c - 1, hp, :], True, True, st, *free)
                    t1.append(tt("dve", inter[:, par::2, :],
                                 psum[:, bx, 0:NH // 2 * (DH + 1)].rearrange("p (h n) -> p h n", n=DH + 1),
                                 dec[:, 0, c, par::2].unsqueeze(2).to_broadcast([P, NH // 2, DH + 1]), ALU.mult,
                                 wx, decd, *numd[-1:]))
                    ring.free(bx, t1[-1])
                numd.append(tt("dve", num[:, c], intra, inter[:], ALU.add, *t1, wi_))
            ring.free(bn, numd[-1])

        numf = num[:].rearrange("p c h n -> p (c h) n")
        n_ = act(nrm[:, 1, :], numf[:, :, DH], ACT.Abs, *numd)
        n0 = tt("dve", nrm[:, 0, :], nrm[:, 1, :], dec[:, 3].rearrange("p c h -> p (c h)"), ALU.max, n_, decd)
        n1_ = ts("dve", nrm[:, 0, :], nrm[:, 0, :], 1e-6, None, ALU.add, None, n0)
        n2_ = q.put("dve", lambda e, b: e.reciprocal(nrm[:, 1, :], nrm[:, 0, :]), n1_)

        def over_head(v):
            return v.unsqueeze(2).to_broadcast([P, NG, DH])

        hd = tt("dve", hh, numf[:, :, 0:DH], over_head(nrm[:, 1, :]), ALU.mult, n2_)
        m1 = red(hm[:, 0, :], hh, ALU.add, hd)
        m2 = ts("dve", hm[:, 0, :], hm[:, 0, :], 1.0 / DH, None, ALU.mult, None, m1)
        hc = tt("dve", hh, hh, over_head(hm[:, 0, :]), ALU.subtract, m2)
        sq = act(hs, hh, ACT.Square, hc)
        v1 = red(hm[:, 1, :], hs, ALU.add, sq)
        v2 = ts("dve", hm[:, 2, :], hm[:, 1, :], 1.0 / DH, 1e-6, ALU.mult, ALU.add, v1)
        v3 = power(hm[:, 3, :], hm[:, 2, :], NG, v2)
        hn = tt("dve", hh, hh, over_head(hm[:, 3, :]), ALU.mult, v3)
        hw = tt("pool", hh.rearrange("p (c h) n -> p c (h n)", c=NT), hh.rearrange("p (c h) n -> p c (h n)", c=NT),
                onw[:].unsqueeze(1).to_broadcast([P, NT, E]), ALU.mult, hn)
        x2d = tt("dve", x2[:], xin[:], hh.rearrange("p (c h) n -> p c (h n)", c=NT), ALU.add, hw)

        mo = moments(x2, x2d)
        r0 = ts("dve", rstd[:, 0, :], mv[:, :, 1], 1e-5, None, ALU.add, None, mo)
        r1 = power(rstd[:, 1, :], rstd[:, 0, :], NT, r0)
        r2 = tt("dve", rstd[:, 2, :], mv[:, :, 1], rstd[:, 1, :], ALU.mult, r1)
        r3 = tt("dve", rstd[:, 2, :], rstd[:, 2, :], rstd[:, 1, :], ALU.mult, r2)
        r4 = ts("dve", rstd[:, 2, :], rstd[:, 2, :], 1e-6, None, ALU.add, None, r3)
        r5 = power(rstd[:, 3, :], rstd[:, 2, :], NT, r4)
        for t in range(NT):
            xfd = ts("dve", xf[:, t, :], x2[:, t, :], mv[:, t, 0:1], rstd[:, 1, t:t + 1], ALU.subtract, ALU.mult, r5)
        for t in range(NT):
            n1d = ts("dve", n1[:, t, :], xf[:, t, :], rstd[:, 3, t:t + 1], None, ALU.mult, None, xfd)
        n1Td = rows_to_columns(n1, lambda c, ps, w: act(n1T[:, c, :], ps, ACT.Identity, w, scale=ln1[:, 0, c:c + 1],
                                                        bias=ln1[:, 1, c:c + 1], accum_out=msum[:, c:c + 1]), n1d)

        def router(src_sum, w_, bias_, n, done):
            sc = ts("dve", src_sum[:], src_sum[:], 1.0 / S, None, ALU.mult, None, *done)
            for c in range(KC):
                bcd = copy("dve", mbc[:, c, :], src_sum[:, c:c + 1].to_broadcast([P, P]), sc)
            br, free = ring.take()
            for c in range(KC):
                w = mm(psum[:, br, 0:n], mbc[:, c, :], w_[:, c, :], c == 0, c == KC - 1, bcd, *free)
            return br, w

        br, w = router(msum, rw, rb, M, n1Td)
        p1 = tt("dve", mp[:], psum[:, br, 0:M], rb[:], ALU.add, w)
        ring.free(br, p1)
        p2 = red(sm1[:, 0:1], mp[:], ALU.max, p1)
        p3 = ts("dve", mp[:], mp[:], sm1[:, 0:1], None, ALU.subtract, None, p2)
        p4 = act(mp[:], mp[:], ACT.Exp, p3)
        p5 = red(sm1[:, 1:2], mp[:], ALU.add, p4)
        p6 = q.put("dve", lambda e, b: e.reciprocal(sm1[:, 2:3], sm1[:, 1:2]), p5)
        mpd = ts("dve", mp[:], mp[:], sm1[:, 2:3], None, ALU.mult, None, p6)

        stored = {}
        loads = []
        slot_free = [None, None]
        n = 0
        for m in range(M):
            for which, (w_, bias_, scale_, terms, stack) in enumerate(
                    ((wk, bk, 1.0, TERMS_K, kst), (wq, bqs, KD ** -0.5, TERMS_Q, qst))):
                sts = []
                for c in range(KC):
                    sl = n % 2
                    n += 1
                    bp, free = ring.take()
                    for kc in range(KC):
                        w = mm(psum[:, bp, :], w_[:, kc, m, c * P:(c + 1) * P], n1T[:, kc, :], kc == 0, kc == KC - 1,
                               *n1Td, *free)
                    f1 = act(proj[:, sl, :], psum[:, bp, :], ACT.Identity, w, slot_free[sl], bias=bias_[:, m, c:c + 1],
                             scale=scale_)
                    ring.free(bp, f1)
                    g1 = copy("dve", parts[:, sl, 0, :], proj[:, sl, :], f1, slot_free[sl])
                    g2 = tt("dve", resid[:, sl, :], proj[:, sl, :], parts[:, sl, 0, :], ALU.subtract, g1)
                    g3 = copy("dve", parts[:, sl, 1, :], resid[:, sl, :], g2)
                    g4 = tt("dve", parts[:, sl, 2, :], resid[:, sl, :], parts[:, sl, 1, :], ALU.subtract, g3)
                    slot_free[sl] = q.dma("sp", f"store_{sl}", lambda e, b, m=m, c=c, sl=sl, which=which: e.dma_start(
                        parts_dram[which, m, c].rearrange("j p s -> p j s"), parts[:, sl, :, :]), g4)
                    sts.append(slot_free[sl])
                for i, j in enumerate(terms):
                    for c in range(KC):
                        ld = q.dma("sp", f"stack_{which}_{m}", lambda e, b, m=m, c=c, i=i, j=j, which=which, stack=stack: e.dma_start(
                            stack[i * KD:(i + 1) * KD, m * H + c * HC:m * H + (c + 1) * HC, :],
                            parts_dram[which, m, c, j].rearrange("(h k) s -> k h s", k=KD)), *sts)
                stored[(which, m)] = ld

        for t in range(NT):
            bvb, free = ring.take()
            for kc in range(KC):
                w = mm(psum[:, bvb, :], n1T[:, kc, t * P:(t + 1) * P], wv[:, kc].rearrange("p m n -> p (m n)"),
                       kc == 0, kc == KC - 1, *n1Td, *free)
            vd = tt("dve", vst[:, t, :, 0:KD], psum[:, bvb, :].rearrange("p (h k) -> p h k", k=KD),
                    bv[:].rearrange("p m (h k) -> p (m h) k", k=KD), ALU.add, w)
            ring.free(bvb, vd)

        free_all = [w for b_ in range(8) for w in ring.busy[b_]]
        sc_free = [free_all, free_all]
        sm_free = [free_all, free_all]
        cx_free = free_all
        tr_free = free_all
        pr_free = [(), ()]
        cs_free = [(), ()]
        mrow_free = [(), ()]
        tile_n = 0
        sm_n = 0
        mxd = {}
        rowd = {}
        expd = {}

        def maxima(qq, j):
            nonlocal sm_n
            h = qq * QUAD + j
            m = h // H
            for t in range(NT):
                i = sm_n % 2
                sm_n += 1
                w = mm(psum[:, 4 + i, :], qst[0:KROWS, h, t * P:(t + 1) * P], kst[0:KROWS, h, :], True, True,
                       stored[(0, m)], stored[(1, m)], *sm_free[i])
                r = red(mx[:, h, t:t + 1], psum[:, 4 + i, :], ALU.max, w)
                sm_free[i] = (r,)
            mxd[qq] = r

        def max_rows(qq):
            nonlocal tr_free
            w = tr(psum[0:QUAD * NT, 7, 0:P], mx[:, qq * QUAD:(qq + 1) * QUAD, :].rearrange("p h t -> p (h t)"), P,
                   mxd[qq], *tr_free)
            i = qq % 2
            a = ts("dve", mrow[:, i, 0, :], psum[0:QUAD * NT, 7, 0:P], -1.0, None, ALU.mult, None, w, *mrow_free[i])
            c_ = stt(mrow[:, i, 1, :], psum[0:QUAD * NT, 7, 0:P], -1.0, mrow[:, i, 0, :], ALU.mult, ALU.subtract, a)
            tr_free = (c_,)
            for r in range(2):
                ld = q.dma("sp", f"rows_{i}", lambda e, b, r=r: e.dma_start(
                    qst[KROWS + r:KROWS + r + 1, qq * QUAD:(qq + 1) * QUAD, :],
                    mrow[:, i, r, :]), c_)
            mrow_free[i] = (ld,)
            rowd[qq] = ld

        def scores(qq, g):
            nonlocal tile_n
            sl = g % 2
            for pair in range(2):
                i = tile_n % 2
                tile_n += 1
                for jj in range(2):
                    h = qq * QUAD + pair * 2 + jj
                    w = mm(psum[:, 2 * i + jj, :], kst[0:KROWS + 2, h, g * P:(g + 1) * P], qst[0:KROWS + 2, h, :],
                           True, True, rowd[qq], *sc_free[i])
                x_ = act(prob[:, sl, pair * 2:pair * 2 + 2, :], psum[:, 2 * i:2 * i + 2, :], ACT.Exp, w, *pr_free[sl])
                sc_free[i] = (x_,)
            expd[(qq, g)] = x_

        def values(qq, g):
            nonlocal cx_free
            sl = g % 2
            for j in range(QUAD):
                h = qq * QUAD + j
                w = mm(psum[32 * j:32 * j + VW, 6, :], vst[:, g, h, :], prob[:, sl, j, :], g == 0, g == NT - 1,
                       expd[(qq, g)], vd, *(cx_free if g == 0 else ()), tile_position=(0, 32 * j))
            pr_free[sl] = (w,)
            return w

        def context(qq, w):
            nonlocal cx_free, tr_free
            i = qq % 2
            m = qq * QUAD // H
            a = act(ctxs[:, i, :], psum[:, 6, :], ACT.Copy, w, *cs_free[i])
            cx_free = (a,)
            for t in range(NT):
                w2_ = tr(psum[:, 7, t * P:(t + 1) * P], ctxs[:, i, t * P:(t + 1) * P], P, a, *tr_free)
            cs_free[i] = (w2_,)
            v = psum[:, 7, :].rearrange("p (t j n) -> p t j n", t=NT, j=QUAD)
            r = q.put("dve", lambda e, b: e.reciprocal(rden[:, i], v[:, :, :, KD]), w2_)
            o = (qq * QUAD) % H * KD
            for t in range(NT):
                c_ = stt(cx[:, t, m, o:o + QUAD * KD].rearrange("p (j k) -> p j k", k=KD), v[:, t, :, 0:KD], mp[:, m:m + 1],
                         rden[:, i, t, :].unsqueeze(2).to_broadcast([P, QUAD, KD]), ALU.mult, ALU.mult, r, mpd)
            tr_free = (c_,)
            return c_

        for j in range(QUAD):
            maxima(0, j)
        max_rows(0)
        for qq in range(NQ):
            for g in range(NT):
                scores(qq, g)
                if qq + 1 < NQ:
                    maxima(qq + 1, g)
                if g > 0:
                    values(qq, g - 1)
            w = values(qq, NT - 1)
            if qq + 1 < NQ:
                max_rows(qq + 1)
            cxd = context(qq, w)

        used = (*sc_free[0], *sc_free[1], *sm_free[0], *sm_free[1], *cx_free, *tr_free)
        for b_ in range(8):
            ring.free(b_, *used)
        cxTd = []
        for m in range(M):
            cxTd += rows_to_columns(cx[:, :, m, :], lambda c, ps, w, m=m: act(cxT[:, m, c, :], ps, ACT.Copy, w), cxd)
        bm0 = ts("dve", mbc[:].rearrange("p c n -> p (c n)"), bo[:, 0, :], mp[:, 0:1], None, ALU.mult, None, mpd, p1)
        bm1 = stt(mbc[:].rearrange("p c n -> p (c n)"), bo[:, 1, :], mp[:, 1:2], mbc[:].rearrange("p c n -> p (c n)"),
                  ALU.mult, ALU.add, bm0)
        x3a = tt("dve", x3[:], xf[:], mbc[:].rearrange("p c n -> p (c n)").unsqueeze(1).to_broadcast([P, NT, E]),
                 ALU.add, bm1)
        for t in range(NT):
            bw, free = ring.take()
            k = 0
            for m in range(M):
                for c in range(KC):
                    w = mm(psum[:, bw, 0:E], cxT[:, m, c, t * P:(t + 1) * P], wo[:, m, c, :], k == 0, k == M * KC - 1,
                           *cxTd, *free)
                    k += 1
            x3d = tt("dve", x3[:, t, :], x3[:, t, :], psum[:, bw, 0:E], ALU.add, w, x3a)
            ring.free(bw, x3d)

        mo = moments(x3, x3d)
        r0 = ts("dve", rstd[:, 0, :], mv[:, :, 1], 1e-6, None, ALU.add, None, mo)
        r1 = power(rstd[:, 1, :], rstd[:, 0, :], NT, r0)
        for t in range(NT):
            n2d = ts("dve", n2[:, t, :], x3[:, t, :], mv[:, t, 0:1], rstd[:, 1, t:t + 1], ALU.subtract, ALU.mult, r1)
        n2Td = rows_to_columns(n2, lambda c, ps, w: act(n2T[:, c, :], ps, ACT.Identity, w, scale=ln2[:, 0, c:c + 1],
                                                        bias=ln2[:, 1, c:c + 1], accum_out=msum[:, c:c + 1]), n2d)
        br, w = router(msum, fr, fb, NX, n2Td)
        p1 = tt("dve", ep[:], psum[:, br, 0:NX], fb[:], ALU.add, w)
        ring.free(br, p1)
        p2 = red(es[:, 0:1], ep[:], ALU.max, p1)
        p3 = ts("dve", ep[:], ep[:], es[:, 0:1], None, ALU.subtract, None, p2)
        p4 = act(ep[:], ep[:], ACT.Exp, p3)
        p4a = red(es[:, 1:2], ep[:], ALU.add, p4)
        p4b = q.put("dve", lambda e, b: e.reciprocal(es[:, 2:3], es[:, 1:2]), p4a)
        p4c = ts("dve", ep[:], ep[:], es[:, 2:3], None, ALU.mult, None, p4b)
        p5 = q.put("dve", lambda e, b: e.max(top[:], ep[:]), p4c)
        topd = q.put("dve", lambda e, b: e.max_index(topi[:], top[:], ep[:]), p5)
        p6 = red(es[:, 3:4], top[:, 0:TOPK], ALU.add, p5)
        p7 = q.put("dve", lambda e, b: e.reciprocal(es[:, 3:4], es[:, 3:4]), p6)
        gated = ts("dve", gate[:], top[:, 0:TOPK], es[:, 3:4], None, ALU.mult, None, p7)
        wl = []

        def fetch(k):
            def fn(e, b, second):
                x_ = e.value_load(topi[0:1, k:k + 1], min_val=0, max_val=NX - 1)
                if second:
                    return e.dma_start(w2[:, k], d["fw2"][bass.ds(x_, 1)].rearrange("o (c p) n -> p (o c) n", p=P))
                return e.dma_start(w1[:, k], d["fw1"][bass.ds(x_, 1)].rearrange("o (c p) n -> p (o c) n", p=P))
            q.dma("sp", f"expert_{k}", lambda e, b: fn(e, b, False), topd)
            return q.dma("sp", f"expert_{k}", lambda e, b: fn(e, b, True), topd)

        wl = [fetch(k) for k in range(TOPK)]
        accd = copy("pool", acc[:], x3[:], x3d)
        accd = tt("pool", acc[:], x3[:], x2[:], ALU.add, accd)
        hfree = ()
        for k in range(TOPK):
            hd_ = []
            for f in range(FC):
                bh, free = ring.take()
                for kc in range(KC):
                    w = mm(psum[:, bh, :], w1[:, k, kc, f * P:(f + 1) * P], n2T[:, kc, :], kc == 0, kc == KC - 1,
                           wl[k], *n2Td, *free)
                hd_.append(act(hT[:, f, :], psum[:, bh, :], ACT.Gelu, w, *hfree))
                ring.free(bh, hd_[-1])
            for t in range(NT):
                be, free = ring.take()
                for f in range(FC):
                    w = mm(psum[:, be, 0:E], hT[:, f, t * P:(t + 1) * P], w2[:, k, f, :], f == 0, f == FC - 1,
                           *hd_, *free)
                accd = stt(acc[:, t, :], psum[:, be, 0:E], gate[:, k:k + 1], acc[:, t, :], ALU.mult, ALU.add, w, gated,
                           accd)
                ring.free(be, accd)
            hfree = (w,)
        stored_out = q.dma("sp", "store_out", lambda e, b: e.dma_start(
            out[bass.ds(b, 1)].rearrange("o (t p) n -> p (o t) n", p=P), acc[:]), accd)
        q.put("sp", lambda e, b: e.nop(), stored_out)

        streams = sorted({s for s, _ in q.counts})
        sems = {s: sem("s_" + s) for s in streams}
        block = ctx.enter_context(nc.Block())

        def run(engine):
            def body(e):
                seen = {}

                def issue(region, b, base):
                    for fn, waits, point in q.items[engine].get(region, []):
                        new = False
                        for w in waits:
                            if seen.get((w.sem_name, region), 0) >= w.count:
                                continue
                            seen[(w.sem_name, region)] = w.count
                            new = True
                            e.wait_ge(sems[w.sem_name], w.count if base is None else base(w.sem_name) + w.count)
                            if base is not None and engine == "sp":
                                e.nop(nofuse=True)
                        if base is not None and new and engine != "sp":
                            e.nop(nofuse=True)
                        ins = fn(e, b)
                        ins.then_inc(sems[point.sem_name], point.unit)

                issue("setup", None, None)
                with e.Fori(0, B) as b:
                    held = {}

                    def base(s):
                        if s not in held:
                            held[s] = e.snap(b * q.total(s, "batch") + q.total(s, "setup"))
                        return held[s]

                    for other in ENGINES:
                        if other != "sp" or q.total("sp", "setup"):
                            e.wait_ge(sems[other], base(other))
                            e.nop(nofuse=True)
                    if engine != "sp":
                        e.wait_ge(sems["weights"], q.total("weights", "setup"))
                    issue("batch", b, base)
            return body

        q.region = "setup"
        q.put("sp", lambda e, b: e.nop(), ready)
        q.put("pe", lambda e, b: e.transpose(psum[:, 0, 0:P], ident[:], ident[:]), consts)
        q.put("act", lambda e, b: e.activation(sm1[:, 3:4], onecol[:], ACT.Copy), consts)
        block.sync(run("sp"))
        block.gpsimd(run("pool"))
        block.scalar(run("act"))
        block.vector(run("dve"))
        block.tensor(run("pe"))


_SHORT = {"x": "x", "ctx_1024": "ctx_1024"}
_PREFIXES = ("L0_xattn_", "L0_ffn_mha_", "L0_ffn_")


def _short(name):
    for p in _PREFIXES:
        if name.startswith(p):
            return name[len(p):]
    return name


def kernel(**inputs):
    import concourse.bacc as _bacc
    from concourse.bass_utils import run_bass_kernel_spmd as _run

    nc = _bacc.Bacc("TRN2", target_bir_lowering=False, num_devices=1)
    arrays, d = {}, {}
    for name in inputs:
        a = np.ascontiguousarray(inputs[name])
        arrays[f"in_{name}"] = a
        d[_short(name)] = nc.dram_tensor(f"in_{name}", a.shape, mybir.dt.from_np(a.dtype), kind="ExternalInput").ap()
    shape = inputs["x"].shape
    out = nc.dram_tensor("out", shape, F32, kind="ExternalOutput").ap()
    build(nc, d, out)
    r = _run(nc, [arrays], core_ids=[0])
    return r.results[0]["out"]
```

```python
from contextlib import ExitStack

import numpy as np
import concourse.bass as bass
from concourse import mybir

F32 = mybir.dt.float32
BF16 = mybir.dt.bfloat16
U32 = mybir.dt.uint32
ALU = mybir.AluOpType
ACT = mybir.ActivationFunctionType
AX = mybir.AxisListType.X

P = 128
ENGINES = ("pe", "act", "dve", "pool", "sp")


class Point:

    def __init__(self, sem_name, region, count, unit):
        self.sem_name, self.region, self.count, self.unit = sem_name, region, count, unit


class Queues:

    def __init__(self):
        self.items = {e: {} for e in ENGINES}
        self.counts = {}
        self.region = None

    def enter(self, region):
        self.region = region

    def _point(self, sem_name, unit):
        key = (sem_name, self.region)
        self.counts[key] = self.counts.get(key, 0) + unit
        return Point(sem_name, self.region, self.counts[key], unit)

    def put(self, engine, fn, *waits):
        point = self._point(engine, 1)
        self.items[engine].setdefault(self.region, []).append((fn, [w for w in waits if w is not None], point))
        return point

    def dma(self, engine, stream, fn, *waits):
        point = self._point(stream, 16)
        self.items[engine].setdefault(self.region, []).append((fn, [w for w in waits if w is not None], point))
        return point

    def total(self, sem_name, region):
        return self.counts.get((sem_name, region), 0)


class Banks:

    def __init__(self, banks):
        self.banks, self.busy, self.order = banks, {b: () for b in banks}, list(banks)

    def take(self):
        bank = self.order.pop(0)
        return bank, self.busy[bank]

    def free(self, bank, *points):
        self.busy[bank] = points
        self.order.append(bank)

    def reset(self):
        assert len(self.order) == len(self.banks)
        self.busy = {b: () for b in self.banks}


def build(nc, d, out):
    B, S, E = d["x"].shape
    NT = S // P
    KC = E // P
    NH = d["ig_bias"].shape[0]
    DH = E // NH
    NG = NH * NT
    M, _, H, KD = d["wq"].shape
    HC = P // KD
    NX = d["ffn_rb"].shape[0]
    FF = d["fw1"].shape[2]
    FC = FF // P
    TOPK = 2
    QUAD = 4
    NQ = M * H // QUAD
    TERMS_K = (0, 0, 1, 1, 0, 2)
    TERMS_Q = (0, 1, 0, 1, 2, 0)
    KROWS = len(TERMS_K) * KD
    VW = KD + 1

    q = Queues()
    ctx = ExitStack()
    with ctx:
        def sb(name, shape, dt=F32):
            return ctx.enter_context(nc.sbuf_tensor(name, shape, dt))

        psum = ctx.enter_context(nc.psum_tensor("psum", [P, 8, 512], F32))

        ident = sb("ident", [P, P])
        onecol = sb("onecol", [P, 1])
        neghalf = sb("neghalf", [P, NG])
        headsel = sb("headsel", [NH, NH, P])
        wgate = sb("wgate", [P, 3 * KC, 2, NH])
        wgkv = sb("wgkv", [P, KC, 2, NH])
        gbias = sb("gbias", [NH, 2])
        onw = sb("onw", [P, E])
        ln1 = sb("ln1", [P, 2, KC])
        ln2 = sb("ln2", [P, 2, KC])
        wq = sb("wq", [P, KC, M, H * KD])
        wk = sb("wk", [P, KC, M, H * KD])
        wv = sb("wv", [P, KC, M, H * KD])
        bq = sb("bq", [P, M, KC])
        bqs = sb("bqs", [P, M, KC])
        bk = sb("bk", [P, M, KC])
        bv = sb("bv", [P, M, H * KD])
        wo = sb("wo", [P, M, KC, E])
        bo = sb("bo", [P, M, E])
        rw = sb("rw", [P, KC, M])
        rb = sb("rb", [P, M])
        fr = sb("fr", [P, KC, NX])
        fb = sb("fb", [P, NX])

        xin = sb("xin", [P, NT, E])
        kin = sb("kin", [P, NT, E])
        vaug = sb("vaug", [P, NT, NH, DH + 1])
        qbuf = sb("qbuf", [P, NG * (DH + 1)])
        qn = qbuf[:, 0:NT * E].rearrange("p (t n) -> p t n", t=NT)
        num = qbuf[:].rearrange("p (c h n) -> p c h n", c=NT, h=NH)
        qT = sb("qT", [P, KC, S])
        kT = sb("kT", [P, KC, S])
        hh = qT[:].rearrange("p c (g d) -> p (c g) d", d=DH)
        hs = kT[:].rearrange("p c (g d) -> p (c g) d", d=DH)
        proj = sb("proj", [P, 2, S])
        resid = sb("resid", [P, 2, S])
        gi, gf = proj[0:NH, 0], proj[0:NH, 1]
        ga, lf = resid[0:NH, 0], resid[0:NH, 1]
        AW = NH * (DH + 1)
        vdec = resid[:].rearrange("p a s -> p (a s)")[:, 0:(NT - 1) * AW].rearrange(
            "p (c h n) -> p c h n", c=NT - 1, h=NH)
        flat = proj[:].rearrange("p a s -> p (a s)")
        inter = flat[:, 0:AW].rearrange("p (h n) -> p h n", h=NH)
        state = flat[:, AW:AW + (NT - 1) * AW // 2].rearrange("p (c h n) -> p c h n", c=NT - 1, h=NH // 2)
        parts = sb("parts", [P, 2, 3, S], BF16)
        rows = parts[0:NH].rearrange("p a j s -> p (a j s)").bitcast(F32).rearrange("p (r s) -> p r s", r=3)
        cols = sb("cols", [P, 3, NT, NH])
        gend = sb("gend", [P, NH, NT])
        dec = sb("dec", [P, 4, NT, NH])
        cmat = sb("cmat", [P, NH, S])
        nrm = sb("nrm", [P, 2, NG])
        hm = sb("hm", [P, 4, NG])
        n1T = sb("n1T", [P, KC, S])
        mp = sb("mp", [P, M])
        kst = sb("kst", [P, M * H, S], BF16)
        qst = sb("qst", [P, M * H, S], BF16)
        vst = sb("vst", [P, NT, M * H, VW])
        mpc = sb("mpc", [P, M])
        mx = sb("mx", [P, M * H, NT])
        mrow = sb("mrow", [QUAD * NT, 2, 2, P], BF16)
        prob = sb("prob", [P, 2, QUAD, S])
        ctxs = sb("ctxs", [P, S])
        rden = sb("rden", [P, NT, QUAD])
        cx = sb("cx", [P, NT, M, H * KD])
        x2k = sb("x2k", [P, NT, E])
        mk = sb("mk", [P, 2, NT])
        bmix = sb("bmix", [P, E])
        x3 = sb("x3", [P, NT, E])
        acc = sb("acc", [P, NT, E])
        cxT = sb("cxT", [P, M, KC, S])
        hT = cxT[:].rearrange("p m c s -> p (m c) s")
        n2T = sb("n2T", [P, KC, S])
        w1 = x3[:].rearrange("p t n -> p (t n)").rearrange("p (c f) -> p c f", c=KC)
        w2 = sb("w2", [P, FC, E])
        ep = sb("ep", [P, NX])
        top = sb("top", [P, NX])
        topi = sb("topi", [P, NX], U32)
        gate = sb("gate", [P, TOPK])

        class Scratch:

            def __init__(self, tag):
                self.stats = sb("stats" + tag, [P, NT, 6])
                self.mv = sb("mv" + tag, [P, NT, 2])
                self.rstd = sb("rstd" + tag, [P, 4, NT])
                self.msum = sb("msum" + tag, [P, KC])
                self.mbc = sb("mbc" + tag, [P, KC, P])
                self.sm = sb("sm" + tag, [P, 4])

        sa, se = Scratch("_a"), Scratch("_e")
        parts_dram = nc.dram_tensor("parts_dram", (2, M, KC, 3, P, S), BF16, kind="Internal").ap()

        def sem(name):
            return ctx.enter_context(nc.semaphore(name))

        q.enter("setup")

        def load(stream, dst, src):
            return q.dma("sp", stream, lambda e, b: e.dma_start(dst, src, allow_slow_non_contiguous=True))

        ldk0 = load("first_ctx", kin[:], d["ctx_1024"][0].rearrange("(t p) n -> p t n", p=P))
        ldx0 = load("first_x", xin[:], d["x"][0].rearrange("(t p) n -> p t n", p=P))

        for g, name in enumerate(("ig_kernel", "fg_kernel")):
            load("w_gates", wgate[:, :, g, :], d[name].rearrange("(c p) h -> p c h", p=P))
            gates_in = load("w_gates", gbias[:, g:g + 1], d[("ig_bias", "fg_bias")[g]].rearrange("(h o) -> h o", o=1))
        load("weights", onw[:], d["outnorm_weight"].rearrange("(o h) d -> o (h d)", o=1).to_broadcast([P, E]))
        for i, t in enumerate((ln1, ln2)):
            for j, s in enumerate("gb"):
                load("weights", t[:, j, :], d[f"ln{i + 1}_{s}"].rearrange("(c p) -> p c", p=P))
        for t, name in ((wq, "wq"), (wk, "wk"), (wv, "wv")):
            for m in range(M):
                load("weights", t[:, :, m, :], d[name][m].rearrange("(c p) h k -> p c (h k)", p=P))
        for t, name in ((bq, "bq"), (bk, "bk")):
            for m in range(M):
                load("weights", t[:, m, :], d[name][m].rearrange("(c h) k -> (h k) c", c=KC))
        load("weights", bv[:], d["bv"].rearrange("(o m) h k -> o m (h k)", o=1).to_broadcast([P, M, H * KD]))
        for m in range(M):
            load("weights", wo[:, m, :, :], d["wo"][m].rearrange("(c h) k n -> (h k) c n", c=KC))
        load("weights", bo[:], d["bo"].rearrange("(o m) n -> o m n", o=1).to_broadcast([P, M, E]))
        load("weights", rw[:], d["rw"].rearrange("(c p) m -> p c m", p=P))
        load("weights", rb[:], d["rb"].rearrange("(o m) -> o m", o=1).to_broadcast([P, M]))
        load("weights", fr[:], d["ffn_rw"].rearrange("(c p) m -> p c m", p=P))
        weights = load("weights", fb[:], d["ffn_rb"].rearrange("(o m) -> o m", o=1).to_broadcast([P, NX]))

        zero = q.put("pool", lambda e, b: e.memset(ident[:], 0.0))
        q.put("pool", lambda e, b: e.affine_select(out=ident[:], in_=ident[:], compare_op=ALU.not_equal, fill=1.0,
                                                   base=0, pattern=[[-1, P]], channel_multiplier=1), zero)
        q.put("pool", lambda e, b: e.memset(onecol[:], 1.0))
        q.put("pool", lambda e, b: e.memset(neghalf[:], -0.5))
        q.put("pool", lambda e, b: e.memset(vaug[:, :, :, DH:DH + 1], 1.0))
        consts = q.put("pool", lambda e, b: e.memset(vst[:, :, :, KD:KD + 1], 1.0))
        q.put("dve", lambda e, b: e.memset(kst[KROWS:KROWS + 2, :, :], 1.0))
        q.put("dve", lambda e, b: e.memset(psum[:, 6, :], 0.0))
        for h in range(NH):
            q.put("dve", lambda e, b, h=h: e.tensor_copy(headsel[:, h, :], ident[0:NH, h:h + 1].to_broadcast([NH, P])),
                  consts)
        q.put("dve", lambda e, b: e.tensor_tensor(wgkv[:], wgate[:, KC:2 * KC], wgate[:, 2 * KC:3 * KC], ALU.add),
              gates_in)

        def mm(out_, lhsT, rhs, start, stop, *waits, **kw):
            return q.put("pe", lambda e, b: e.matmul(out_, lhsT, rhs, start=start, stop=stop, **kw), *waits)

        def tr(out_, in_, n, *waits):
            return q.put("pe", lambda e, b: e.transpose(out_, in_, ident[0:n, 0:n]), *waits)

        def act(out_, in_, f, *waits, **kw):
            return q.put("act", lambda e, b: e.activation(out_, in_, f, **kw), *waits)

        def tt(eng, out_, a, c, op, *waits):
            return q.put(eng, lambda e, b: e.tensor_tensor(out_, a, c, op), *waits)

        def ts(eng, out_, a, s1, s2, op0, op1, *waits):
            if op1 is None:
                return q.put(eng, lambda e, b: e.tensor_scalar(out_, a, s1, None, op0), *waits)
            return q.put(eng, lambda e, b: e.tensor_scalar(out_, a, s1, s2, op0, op1), *waits)

        def stt(out_, a, s, c, op0, op1, *waits):
            return q.put("dve", lambda e, b: e.scalar_tensor_tensor(out=out_, in0=a, scalar=s, in1=c,
                                                                    op0=op0, op1=op1), *waits)

        def red(out_, in_, op, *waits):
            return q.put("dve", lambda e, b: e.tensor_reduce(out_, in_, AX, op), *waits)

        def copy(eng, out_, in_, *waits):
            return q.put(eng, lambda e, b: e.tensor_copy(out_, in_), *waits)

        def power(out_, in_, n, *waits):
            return q.put("pool", lambda e, b: e.tensor_tensor(out_, in_, neghalf[:, 0:n], ALU.pow), *waits)

        ring = Banks((5, 7, 4))

        def moments(sc, src, *waits):
            for t in range(NT):
                a = q.put("dve", lambda e, b, t=t: e.bn_stats(sc.stats[:, t, :], src[:, t, :]), *waits)
            for t in range(NT):
                last = q.put("dve", lambda e, b, t=t: e.bn_aggr(sc.mv[:, t, :], sc.stats[:, t, :]), a)
            return last

        def chunk_to_columns(src, c, evacuate, *waits):
            bk_, free = ring.take()
            for t in range(NT):
                last = tr(psum[:, bk_, t * P:(t + 1) * P], src[:, t, c * P:(c + 1) * P], P, *waits, *free)
            done = evacuate(c, psum[:, bk_, :], last)
            ring.free(bk_, done)
            return done

        def mean_columns(sc, *done):
            s_ = ts("dve", sc.msum[:], sc.msum[:], 1.0 / S, None, ALU.mult, None, *done)
            return copy("dve", sc.mbc[:], sc.msum[:].unsqueeze(2).to_broadcast([P, KC, P]), s_)

        def logits(sc, dst, w_, bias_, n, bcd):
            br, free = ring.take()
            for c in range(KC):
                w = mm(psum[:, br, 0:n], sc.mbc[:, c, :], w_[:, c, :], c == 0, c == KC - 1, bcd, *free)
            p1 = tt("dve", dst[:], psum[:, br, 0:n], bias_[:], ALU.add, w)
            ring.free(br, p1)
            return p1

        def softmax(sc, v, p1):
            p2 = red(sc.sm[:, 0:1], v[:], ALU.max, p1)
            p3 = ts("dve", v[:], v[:], sc.sm[:, 0:1], None, ALU.subtract, None, p2)
            p4 = act(v[:], v[:], ACT.Exp, p3)
            p5 = red(sc.sm[:, 1:2], v[:], ALU.add, p4)
            p6 = q.put("dve", lambda e, b: e.reciprocal(sc.sm[:, 2:3], sc.sm[:, 1:2]), p5)
            return ts("dve", v[:], v[:], sc.sm[:, 2:3], None, ALU.mult, None, p6)

        def stage_a(ahead, late, x_free, n1T_free, stack_free, vst_free, result):
            ldk = ldk0 if ahead == 0 else q.dma("sp", "load_ctx", lambda e, b: e.dma_start(
                kin[:], d["ctx_1024"][bass.ds(b + ahead, 1)].rearrange("o (t p) n -> p (o t) n", p=P)))
            vcopy = copy("pool", vaug[:, :, :, 0:DH], kin[:].rearrange("p t (h d) -> p t h d", h=NH), ldk)
            yield
            kTd = []
            for c in range(KC):
                kTd.append(chunk_to_columns(kin, c, lambda c, ps, w: act(kT[:, c, :], ps, ACT.Copy, w), ldk))
                yield
            while x_free and not x_free[0]:
                yield
            ldx = ldx0 if ahead == 0 else q.dma("sp", "load_x", lambda e, b: e.dma_start(
                xin[:], d["x"][bass.ds(b + ahead, 1)].rearrange("o (t p) n -> p (o t) n", p=P)), *(x_free or ()))
            yield
            mo = moments(sa, xin, ldx)
            e1 = ts("dve", sa.rstd[:, 0, :], sa.mv[:, :, 1], 1e-5, None, ALU.add, None, mo)
            pw = power(sa.rstd[:, 1, :], sa.rstd[:, 0, :], NT, e1)
            yield
            for t in range(NT):
                qdone = ts("dve", qn[:, t, :], xin[:, t, :], sa.mv[:, t, 0:1], sa.rstd[:, 1, t:t + 1],
                           ALU.subtract, ALU.mult, pw)
            yield
            qTd = []
            for c in range(KC):
                qTd.append(chunk_to_columns(qn, c, lambda c, ps, w: act(qT[:, c, :], ps, ACT.Copy, w), qdone))
                yield

            gates = []
            for g in range(2):
                bk_, free = ring.take()
                for c in range(KC):
                    mm(psum[0:NH, bk_, :], wgkv[:, c, g, :], kT[:, c, :], c == 0, False, *kTd, *free)
                for c in range(KC):
                    last = mm(psum[0:NH, bk_, :], wgate[:, c, g, :], qT[:, c, :], False, c == KC - 1, *qTd)
                gates.append(act((gi, gf)[g], psum[0:NH, bk_, :], ACT.Identity, last, bias=gbias[:, g:g + 1]))
                ring.free(bk_, gates[-1])
                yield
            igd, fgd = gates
            a1 = act(ga, gf, ACT.Abs, fgd)
            a2 = act(ga, ga, ACT.Exp, a1, scale=-1.0)
            a3 = act(ga, ga, ACT.Ln, a2, bias=onecol[0:NH, :])
            yield
            lfd = stt(lf, gf, 0.0, ga, ALU.min, ALU.subtract, a3)
            Fd = q.put("dve", lambda e, b: e.tensor_tensor_scan(gf, onecol[0:NH].to_broadcast([NH, S]), lf, 0.0, ALU.mult, ALU.add), lfd)
            gd = tt("dve", rows[:, 0, :], gi, gf, ALU.subtract, Fd, igd)
            yield
            Gd = q.put("dve", lambda e, b: e.tensor_tensor_scan(rows[:, 1, :], rows[:, 0, :], rows[:, 0, :], -3.0e38,
                                                                ALU.max, ALU.max), gd)
            Md = tt("dve", rows[:, 2, :], gf, rows[:, 1, :], ALU.add, Gd)
            yield

            bc, free = ring.take()
            for r in range(3):
                for c in range(NT):
                    o = (r * NT + c) * NH
                    last = tr(psum[:, bc, o:o + NH], rows[:, r, c * P:(c + 1) * P], NH, Md, *free)
            cold = copy("dve", cols[:].rearrange("p r c h -> p (r c h)"), psum[:, bc, 0:3 * NG], last)
            ring.free(bc, cold)
            yield
            masked, gends = [], []
            for h in range(NH):
                bg, free = ring.take()
                w = mm(psum[:, bg, :], headsel[:, h, :], rows[:, 1, :], True, True, Md, *free)
                gends.append(copy("dve", gend[:, h, :], psum[:, bg, P - 1::P], w))
                for c in range(NT):
                    last = act(cmat[:, h, c * P:(c + 1) * P], psum[:, bg, c * P:(c + 1) * P], ACT.Exp, w, cold,
                               gends[-1], bias=cols[:, 0, c, h:h + 1], scale=-1.0)
                ring.free(bg, last)
                dview = cmat[:, h, :].rearrange("p (c s) -> p c s", c=NT)
                masked.append(q.put("pool", lambda e, b, v=dview: e.affine_select(
                    out=v, in_=v, compare_op=ALU.is_ge, fill=0.0, base=0, pattern=[[0, NT], [1, P]],
                    channel_multiplier=-1), last))
                yield

            ge = gend[:].rearrange("p h c -> p c h")
            tt("dve", dec[:, 0, 1:NT, :], ge[:, 0:NT - 1, :], cols[:, 1, 1:NT, :], ALU.subtract, *gends, cold)
            tt("dve", dec[:, 1, 0:NT - 1, :], cols[:, 0, 0:NT - 1, :], ge[:, 0:NT - 1, :], ALU.subtract)
            tt("dve", dec[:, 2, 1:NT - 1, :], ge[:, 0:NT - 2, :], ge[:, 1:NT - 1, :], ALU.subtract)
            dd = ts("dve", dec[:, 3, :, :], cols[:, 2, :, :], -1.0, None, ALU.mult, None)
            yield
            act(dec[:, 0, 1:NT, :], dec[:, 0, 1:NT, :], ACT.Exp, dd)
            act(dec[:, 1, 0:NT - 1, :], dec[:, 1, 0:NT - 1, :], ACT.Exp)
            act(dec[:, 2, 1:NT - 1, :], dec[:, 2, 1:NT - 1, :], ACT.Exp)
            decd = act(dec[:, 3, :, :], dec[:, 3, :, :], ACT.Exp)
            wsc = ts("dve", dec[:, 1, 0:NT - 1, :], dec[:, 1, 0:NT - 1, :], DH ** -0.5, None, ALU.mult, None, decd)
            vw = tt("pool", vdec, vaug[:, 0:NT - 1],
                    dec[:, 1, 0:NT - 1, :].unsqueeze(3).to_broadcast([P, NT - 1, NH, DH + 1]), ALU.mult, wsc, vcopy)
            yield

            cd = []
            for h in range(NH):
                ba, free = ring.take()
                o = DH * (h % 2)
                for c in range(NT):
                    s_ = slice(c * P, (c + 1) * P)
                    last = mm(psum[:, ba, s_], kT[o:o + DH, h // 2, s_], qT[o:o + DH, h // 2, s_], True, True,
                              *qTd, *kTd, *free)
                cd.append(stt(cmat[:, h, :], psum[:, ba, :], DH ** -0.5, cmat[:, h, :], ALU.mult, ALU.mult, last,
                              masked[h]))
                ring.free(ba, cd[-1])
                yield

            st = None
            for c in range(NT - 1):
                bs, free = ring.take()
                for h in range(NH):
                    o = DH * (h % 2)
                    last = mm(psum[o:o + DH, bs, (h // 2) * (DH + 1):(h // 2 + 1) * (DH + 1)],
                              kin[:, c, h * DH:(h + 1) * DH], vdec[:, c, h, :], True, True, vw, *free)
                if c == 0:
                    st = copy("dve", state[:, 0, :, :].rearrange("p a n -> p (a n)"),
                              psum[:, bs, 0:(NH // 2) * (DH + 1)], last)
                else:
                    prev = st
                    for h in range(NH):
                        o = DH * (h % 2)
                        st = stt(state[o:o + DH, c, h // 2, :], state[o:o + DH, c - 1, h // 2, :],
                                 dec[o:o + DH, 2, c, h:h + 1],
                                 psum[o:o + DH, bs, (h // 2) * (DH + 1):(h // 2 + 1) * (DH + 1)],
                                 ALU.mult, ALU.add, last, prev, decd)
                ring.free(bs, st)
                yield

            numd = []
            for c in range(NT):
                s_ = slice(c * P, (c + 1) * P)
                bn, free = ring.take()
                for h in range(NH):
                    wi_ = mm(psum[:, bn, h * (DH + 1):(h + 1) * (DH + 1)], cmat[:, h, s_], vaug[:, c, h, :], True, True,
                             *cd, vcopy, *free)
                intra = psum[:, bn, 0:NH * (DH + 1)].rearrange("p (h n) -> p h n", h=NH)
                if c == 0:
                    numd.append(copy("dve", num[:, c], intra, wi_))
                else:
                    t1 = []
                    for par in range(2):
                        bx, free = ring.take()
                        o = DH * par
                        for hp in range(NH // 2):
                            wx = mm(psum[:, bx, hp * (DH + 1):(hp + 1) * (DH + 1)], qT[o:o + DH, hp, s_],
                                    state[o:o + DH, c - 1, hp, :], True, True, st, *free)
                        t1.append(tt("dve", inter[:, par::2, :],
                                     psum[:, bx, 0:NH // 2 * (DH + 1)].rearrange("p (h n) -> p h n", n=DH + 1),
                                     dec[:, 0, c, par::2].unsqueeze(2).to_broadcast([P, NH // 2, DH + 1]), ALU.mult,
                                     wx, decd, *numd[-1:]))
                        ring.free(bx, t1[-1])
                    numd.append(tt("dve", num[:, c], intra, inter, ALU.add, *t1, wi_))
                ring.free(bn, numd[-1])
                yield

            numf = num.rearrange("p c h n -> p (c h) n")
            n_ = act(nrm[:, 1, :], numf[:, :, DH], ACT.Abs, *numd)
            n0 = tt("dve", nrm[:, 0, :], nrm[:, 1, :], dec[:, 3].rearrange("p c h -> p (c h)"), ALU.max, n_, decd)
            n1_ = ts("dve", nrm[:, 0, :], nrm[:, 0, :], 1e-6, None, ALU.add, None, n0)
            n2_ = q.put("dve", lambda e, b: e.reciprocal(nrm[:, 1, :], nrm[:, 0, :]), n1_)

            def over_head(v):
                return v.unsqueeze(2).to_broadcast([P, NG, DH])

            hd = tt("dve", hh, numf[:, :, 0:DH], over_head(nrm[:, 1, :]), ALU.mult, n2_)
            m1 = red(hm[:, 0, :], hh, ALU.add, hd)
            m2 = ts("dve", hm[:, 0, :], hm[:, 0, :], 1.0 / DH, None, ALU.mult, None, m1)
            yield
            hc = tt("pool", hh, hh, over_head(hm[:, 0, :]), ALU.subtract, m2)
            sq = act(hs, hh, ACT.Square, hc)
            yield
            v1 = red(hm[:, 1, :], hs, ALU.add, sq)
            v2 = ts("dve", hm[:, 2, :], hm[:, 1, :], 1.0 / DH, 1e-6, ALU.mult, ALU.add, v1)
            v3 = power(hm[:, 3, :], hm[:, 2, :], NG, v2)
            hv = hh.rearrange("p (c h) n -> p c (h n)", c=NT)
            hw = tt("pool", hs.rearrange("p (c h) n -> p c (h n)", c=NT), hv,
                    onw[:].unsqueeze(1).to_broadcast([P, NT, E]), ALU.mult, v1, *late)
            yield
            hn = tt("dve", hh, hs, over_head(hm[:, 3, :]), ALU.mult, v3, hw)
            yield
            x2d = tt("pool", xin[:], xin[:], hv, ALU.add, hn)
            yield

            mo = moments(sa, xin, x2d)
            r0 = ts("dve", sa.rstd[:, 0, :], sa.mv[:, :, 1], 1e-5, None, ALU.add, None, mo)
            r1 = power(sa.rstd[:, 1, :], sa.rstd[:, 0, :], NT, r0)
            yield
            r2 = tt("dve", sa.rstd[:, 2, :], sa.mv[:, :, 1], sa.rstd[:, 1, :], ALU.mult, r1)
            r3 = tt("dve", sa.rstd[:, 2, :], sa.rstd[:, 2, :], sa.rstd[:, 1, :], ALU.mult, r2)
            r4 = ts("dve", sa.rstd[:, 2, :], sa.rstd[:, 2, :], 1e-6, None, ALU.add, None, r3)
            r5 = power(sa.rstd[:, 3, :], sa.rstd[:, 2, :], NT, r4)
            r6 = tt("pool", sa.rstd[:, 3, :], sa.rstd[:, 3, :], sa.rstd[:, 1, :], ALU.mult, r5)
            yield
            for t in range(NT):
                n1d = ts("dve", qn[:, t, :], xin[:, t, :], sa.mv[:, t, 0:1], sa.rstd[:, 3, t:t + 1],
                         ALU.subtract, ALU.mult, r6)
            yield
            n1Td = []
            for c in range(KC):
                n1Td.append(chunk_to_columns(qn, c, lambda c, ps, w: act(
                    n1T[:, c, :], ps, ACT.Identity, w, *n1T_free, *late, scale=ln1[:, 0, c:c + 1], bias=ln1[:, 1, c:c + 1],
                    accum_out=sa.msum[:, c:c + 1]), n1d))
                yield

            if late:
                n1Td.append(ts("dve", bqs[:], bq[:], KD ** -0.5, None, ALU.mult, None, *late))

            slot_free = [None, None]
            n = 0
            for m in range(M):
                for which, (w_, bias_, scale_) in enumerate(((wk, bk, 1.0), (wq, bqs, KD ** -0.5))):
                    sts = []
                    for c in range(KC):
                        sl = n % 2
                        n += 1
                        bp, free = ring.take()
                        for kc in range(KC):
                            w = mm(psum[:, bp, :], w_[:, kc, m, c * P:(c + 1) * P], n1T[:, kc, :], kc == 0, kc == KC - 1,
                                   *n1Td, *late, *free)
                        f1 = act(proj[:, sl, :], psum[:, bp, :], ACT.Identity, w, slot_free[sl], bias=bias_[:, m, c:c + 1],
                                 scale=scale_)
                        f2 = act(parts[:, sl, 0, :], psum[:, bp, :], ACT.Identity, w, slot_free[sl],
                                 bias=bias_[:, m, c:c + 1], scale=scale_)
                        ring.free(bp, f2)
                        g2 = tt("dve", resid[:, sl, :], proj[:, sl, :], parts[:, sl, 0, :], ALU.subtract, f1, f2)
                        g3 = copy("dve", parts[:, sl, 1, :], resid[:, sl, :], g2)
                        g4 = tt("dve", parts[:, sl, 2, :], resid[:, sl, :], parts[:, sl, 1, :], ALU.subtract, g3)
                        slot_free[sl] = q.dma("sp", f"store_{sl}", lambda e, b, m=m, c=c, sl=sl, which=which: e.dma_start(
                            parts_dram[which, m, c].rearrange("j p s -> p j s"), parts[:, sl, :, :]), g4)
                        sts.append(slot_free[sl])
                        yield
                    if m == 0:
                        while stack_free and not stack_free[0]:
                            yield
                        result[which] = load_stack(which, 0, *sts, *(stack_free or ()))
                if m == 0:
                    while vst_free and not vst_free[0]:
                        yield
                    for pt in range(NT // 2):
                        project_v(0, pt, *n1Td, *(vst_free or ()))
                        yield
                    bcd = mean_columns(sa, *n1Td)
                    yield
                    p1 = logits(sa, mp, rw, rb, M, bcd)
                    softmax(sa, mp, p1)
                    yield

        def load_stack(which, m, *waits):
            for i, j in enumerate((TERMS_K, TERMS_Q)[which]):
                for c in range(KC):
                    ld = q.dma("sp", f"stack_{which}_{m}", lambda e, b, c=c, i=i, j=j: e.dma_start(
                        (kst, qst)[which][i * KD:(i + 1) * KD, m * H + c * HC:m * H + (c + 1) * HC, :],
                        parts_dram[which, m, c, j].rearrange("(h k) s -> k h s", k=KD)), *waits)
            return ld

        def project_v(m, pt, *waits):
            bvb, free = ring.take()
            for i in range(2):
                t = 2 * pt + i
                for kc in range(KC):
                    w = mm(psum[:, bvb, i * H * KD:(i + 1) * H * KD], n1T[:, kc, t * P:(t + 1) * P], wv[:, kc, m, :],
                           kc == 0, kc == KC - 1, *waits, *free)
            v_ = psum[:, bvb, :].rearrange("p (t h k) -> p t h k", t=2, k=KD)
            for i in range(2):
                vd = tt("dve", vst[:, 2 * pt + i, m * H:(m + 1) * H, 0:KD], v_[:, i],
                        bv[:, m].rearrange("p (h k) -> p h k", k=KD), ALU.add, w)
            ring.free(bvb, vd)
            return w, vd

        def stage_c(behind, points):
            cxTd = []
            for m in range(M):
                for c in range(KC):
                    cxTd.append(chunk_to_columns(cx[:, :, m, :], c, lambda c, ps, w, m=m: act(
                        cxT[:, m, c, :], ps, ACT.Copy, w)))
            points["cx_read"] = cxTd[-1]
            yield
            for t in range(NT):
                xfd = ts("dve", x3[:, t, :], x2k[:, t, :], mk[:, 0, t:t + 1], mk[:, 1, t:t + 1], ALU.subtract, ALU.mult)
            x3a = tt("pool", x3[:], x3[:], bmix[:].unsqueeze(1).to_broadcast([P, NT, E]), ALU.add, xfd)
            points["bmix_read"] = x3a
            for pt in range(NT // 2):
                bw, free = ring.take()
                for i in range(2):
                    k = 0
                    for m in range(M):
                        for c in range(KC):
                            w = mm(psum[:, bw, i * E:(i + 1) * E], cxT[:, m, c, (2 * pt + i) * P:(2 * pt + i + 1) * P],
                                   wo[:, m, c, :], k == 0, k == M * KC - 1, *cxTd, *free)
                            k += 1
                x3d = tt("dve", x3[:, 2 * pt:2 * pt + 2, :].rearrange("p t n -> p (t n)"),
                         x3[:, 2 * pt:2 * pt + 2, :].rearrange("p t n -> p (t n)"), psum[:, bw, :], ALU.add, w, x3a)
                ring.free(bw, x3d)
                yield
            wo_read = w
            accd = tt("pool", acc[:], x3[:], x2k[:], ALU.add, x3d)
            points["x2k_read"] = accd

            mo = moments(se, x3, x3d)
            r0 = ts("dve", se.rstd[:, 0, :], se.mv[:, :, 1], 1e-6, None, ALU.add, None, mo)
            r1 = power(se.rstd[:, 1, :], se.rstd[:, 0, :], NT, r0)
            yield
            for t in range(NT):
                n2d = ts("dve", x3[:, t, :], x3[:, t, :], se.mv[:, t, 0:1], se.rstd[:, 1, t:t + 1],
                         ALU.subtract, ALU.mult, r1, accd)
            yield
            n2Td = []
            for c in range(KC):
                n2Td.append(chunk_to_columns(x3, c, lambda c, ps, w: act(
                    n2T[:, c, :], ps, ACT.Identity, w, scale=ln2[:, 0, c:c + 1], bias=ln2[:, 1, c:c + 1],
                    accum_out=se.msum[:, c:c + 1]), n2d))
                yield
            bcd = mean_columns(se, *n2Td)
            yield
            p1 = logits(se, ep, fr, fb, NX, bcd)
            p4 = softmax(se, ep, p1)
            yield
            p5 = q.put("dve", lambda e, b: e.max(top[:], ep[:]), p4)
            topd = q.put("dve", lambda e, b: e.max_index(topi[:], top[:], ep[:]), p5)
            p6 = red(se.sm[:, 3:4], top[:, 0:TOPK], ALU.add, p5)
            p7 = q.put("dve", lambda e, b: e.reciprocal(se.sm[:, 3:4], se.sm[:, 3:4]), p6)
            gated = ts("dve", gate[:], top[:, 0:TOPK], se.sm[:, 3:4], None, ALU.mult, None, p7)
            yield

            def fetch(k, tag, dst, src, *waits):
                def fn(e, b):
                    x_ = e.value_load(topi[0:1, k:k + 1], min_val=0, max_val=NX - 1)
                    return e.dma_start(dst[:], src[bass.ds(x_, 1)].rearrange("o (c p) n -> p (o c) n", p=P))
                return q.dma("sp", f"expert_{tag}", fn, topd, *waits)

            w1d = fetch(0, "w1", w1, d["fw1"], *n2Td)
            w2d = fetch(0, "w2", w2, d["fw2"])
            yield
            yield
            yield
            hfree = (wo_read,)
            for k in range(TOPK):
                hd_ = []
                for f in range(FC):
                    bh, free = ring.take()
                    for kc in range(KC):
                        w = mm(psum[:, bh, :], w1[:, kc, f * P:(f + 1) * P], n2T[:, kc, :], kc == 0, kc == KC - 1,
                               w1d, *n2Td, *free)
                    hd_.append(act(hT[:, f, :], psum[:, bh, :], ACT.Gelu, w, *hfree))
                    ring.free(bh, hd_[-1])
                if k + 1 < TOPK:
                    w1d = fetch(k + 1, "w1", w1, d["fw1"], w)
                yield
                for pt in range(NT // 2):
                    be, free = ring.take()
                    for i in range(2):
                        t = 2 * pt + i
                        for f in range(FC):
                            w = mm(psum[:, be, i * E:(i + 1) * E], hT[:, f, t * P:(t + 1) * P], w2[:, f, :], f == 0,
                                   f == FC - 1, *hd_, w2d, *free)
                    av = acc[:, 2 * pt:2 * pt + 2, :].rearrange("p t n -> p (t n)")
                    accd = stt(av, psum[:, be, :], gate[:, k:k + 1], av, ALU.mult, ALU.add, w, gated, accd)
                    ring.free(be, accd)
                    yield
                hfree = (w,)
                if k + 1 < TOPK:
                    w2d = fetch(k + 1, "w2", w2, d["fw2"], w)
            points["out"] = q.dma("sp", "store_out", lambda e, b: e.dma_start(
                out[bass.ds(b - behind, 1)].rearrange("o (t p) n -> p (o t) n", p=P), acc[:]), accd)

        class Attention:
            def __init__(self):
                self.sc_free, self.sm_free = [(), ()], [(), ()]
                self.cx_free, self.pr_free, self.cs_free, self.rd_free = (), [(), ()], (), ()
                self.mrow_free = [(), ()]
                self.tile_n = self.sm_n = 0
                self.mxd, self.rowd, self.expd, self.scored = {}, {}, {}, {}

            def maximum(self, qq, j, t, *waits):
                h = qq % NQ * QUAD + j
                i = self.sm_n % 2
                self.sm_n += 1
                w = mm(psum[:, 2 + i, :], qst[0:KROWS, h, t * P:(t + 1) * P], kst[0:KROWS, h, :], True, True,
                       *waits, *self.sm_free[i])
                r = red(mx[:, h, t:t + 1], psum[:, 2 + i, :], ALU.max, w)
                self.sm_free[i] = (r,)
                self.mxd[qq] = r

            def max_rows(self, qq, *waits):
                n = qq % NQ
                bk_, free = ring.take()
                src = psum[0:QUAD * NT, bk_, 0:P]
                w = tr(src, mx[:, n * QUAD:(n + 1) * QUAD, :].rearrange("p h t -> p (h t)"), P, self.mxd[qq], *free)
                i = qq % 2
                a = ts("dve", mrow[:, i, 0, :], src, -1.0, None, ALU.mult, None, w, *self.mrow_free[i])
                c_ = stt(mrow[:, i, 1, :], src, -1.0, mrow[:, i, 0, :], ALU.mult, ALU.subtract, a)
                ring.free(bk_, c_)
                for r in range(2):
                    ld = q.dma("sp", f"rows_{i}", lambda e, b, r=r: e.dma_start(
                        qst[KROWS + r:KROWS + r + 1, n * QUAD:(n + 1) * QUAD, :], mrow[:, i, r, :]), c_, *waits)
                self.mrow_free[i] = (ld,)
                self.rowd[qq] = ld

            def score(self, qq, g, j):
                sl = g % 2
                i = self.tile_n % 2
                self.tile_n += 1
                h = qq * QUAD + j
                w = mm(psum[:, i, :], kst[0:KROWS + 2, h, g * P:(g + 1) * P], qst[0:KROWS + 2, h, :],
                       True, True, self.rowd.get(qq), *self.sc_free[i])
                x_ = act(prob[:, sl, j, :], psum[:, i, :], ACT.Exp, w, *self.pr_free[sl])
                self.sc_free[i] = (x_,)
                self.expd[(qq, g)] = x_
                self.scored[qq] = w

            def values(self, qq, g, *waits):
                sl = g % 2
                for j in range(QUAD):
                    h = qq * QUAD + j
                    w = mm(psum[32 * j:32 * j + VW, 6, :], vst[:, g, h, :], prob[:, sl, j, :], g == 0, g == NT - 1,
                           self.expd[(qq, g)], *waits, *(self.cx_free if g == 0 else ()), tile_position=(0, 32 * j))
                self.pr_free[sl] = (w,)
                return w

            def copy_context(self, w):
                self.copied = act(ctxs[:], psum[:, 6, :], ACT.Copy, w, *self.cs_free)
                self.cx_free = (self.copied,)

            def context(self, qq, *waits):
                m = qq * QUAD // H
                bk_, free = ring.take()
                for t in range(NT):
                    w = tr(psum[:, bk_, t * P:(t + 1) * P], ctxs[:, t * P:(t + 1) * P], P, self.copied, *free)
                self.cs_free = (w,)
                v = psum[:, bk_, :].rearrange("p (t j n) -> p t j n", t=NT, j=QUAD)
                r = q.put("dve", lambda e, b: e.reciprocal(rden[:], v[:, :, :, KD]), w, *self.rd_free)
                o = (qq * QUAD) % H * KD
                c_ = stt(cx[:, :, m, o:o + QUAD * KD].rearrange("p t (j k) -> p t j k", k=KD), v[:, :, :, 0:KD],
                         mpc[:, m:m + 1], rden[:].unsqueeze(3).to_broadcast([P, NT, QUAD, KD]), ALU.mult, ALU.mult,
                         r, *waits)
                self.rd_free = (c_,)
                ring.free(bk_, c_)

        def finish(*points):
            q.put("sp", lambda e, b: e.nop(), *points)

        A_PER, C_PER = 1, 1

        def region(name, with_c, with_a):
            q.enter(name)
            ring.reset()
            at = Attention()
            points, result = {}, {}
            x_free, stack_free, vst_free, n1T_free = [], [], [], []
            mpd = copy("dve", mpc[:], mp[:])
            s1 = [load_stack(which, 1) for which in range(2)]
            stage1 = stage_c(1, points) if with_c else iter(())

            def carry():
                c1 = copy("pool", x2k[:], xin[:], points.get("x2k_read"))
                copy("pool", mk[:, 0, :], sa.mv[:, :, 0], points.get("x2k_read"))
                c2 = copy("pool", mk[:, 1, :], sa.rstd[:, 1, :])
                b0 = ts("dve", bmix[:], bo[:, 0, :], mpc[:, 0:1], None, ALU.mult, None, mpd, points.get("bmix_read"))
                stt(bmix[:], bo[:, 1, :], mpc[:, 1:2], bmix[:], ALU.mult, ALU.add, b0)
                return c2

            def second_values():
                for pt in range(NT // 2):
                    w, points["v1"] = project_v(1, pt)
                    yield
                n1T_free.append(w)

            a_waits = {"x": [], "stack": [], "vst": [], "n1T": n1T_free}
            stage_v = second_values()
            stage2 = stage_a(1, (), a_waits["x"], n1T_free, a_waits["stack"], a_waits["vst"], result) if with_a else iter(())
            carried = False

            def step(gen):
                try:
                    next(gen)
                    return True
                except StopIteration:
                    return False

            if with_a:
                a_waits["x"].append(None)
                a_waits["stack"].append(None)
                a_waits["vst"].append(None)
            if with_c:
                step(stage1)
            sub = 0
            for qq in range(NQ):
                for g in range(NT):
                    slot = qq * NT + g
                    for j in range(QUAD):
                        at.score(qq, g, j)
                        if qq == 0:
                            k = slot * 8 + 2 * j
                            for kk in (k, k + 1):
                                at.maximum(1 + kk // 16, kk % 16 // 4, kk % 4, *(s1 if 1 + kk // 16 >= NQ // 2 else ()))
                        elif qq + 2 < NQ:
                            at.maximum(qq + 2, g, j, *(s1 if qq + 2 >= NQ // 2 else ()))
                        elif qq == NQ - 1 and with_a:
                            at.maximum(NQ, g, j, result[0], result[1])
                        if j % 2:
                            if j == 1 and not step(stage_v) and False:
                                pass
                            if j == 1:
                                for _ in range(C_PER):
                                    step(stage1)
                            if not carried and (not with_c or "x2k_read" in points):
                                carried = True
                                c2 = carry()
                                if with_a:
                                    a_waits["x"][0] = c2
                            if with_a:
                                for _ in range(A_PER):
                                    step(stage2)
                            sub += 1
                    if slot == 0:
                        pass
                    elif g > 0:
                        at.values(qq, g - 1, *((points["v1"],) if qq >= NQ // 2 else ()))
                    else:
                        w = at.values(qq - 1, NT - 1)
                        at.copy_context(w)
                    if g == 1 and qq > 0:
                        at.context(qq - 1, points.get("cx_read"), mpd)
                    if g == 0 and qq == 0 and False:
                        pass
                    if qq == 0 and g == 2:
                        at.max_rows(1)
                    if qq == 1 and g == 0:
                        at.max_rows(2)
                    if qq > 1 and g == 0 and qq + 1 < NQ:
                        at.max_rows(qq + 1)
                    if with_a and slot == NQ // 2 * NT:
                        a_waits["stack"][0] = at.scored[NQ // 2 - 1]
                        a_waits["vst"][0] = w
                if qq == NQ - 2 and with_a:
                    while step(stage2) and (0 not in result or 1 not in result):
                        pass
            w = at.values(NQ - 1, NT - 1, points["v1"])
            at.copy_context(w)
            if with_a:
                at.max_rows(NQ, a_waits["stack"][0])
            at.context(NQ - 1, points.get("cx_read"), mpd)
            for gen in (stage1, stage2):
                while step(gen):
                    pass
            finish(points.get("out"), *at.mrow_free[0], *at.mrow_free[1], *s1,
                   *(Point(f"store_{i}", name, q.total(f"store_{i}", name), 16) for i in range(2) if with_a))

        q.enter("start")
        result = {}
        for _ in stage_a(0, (weights,), [], [], [], [], result):
            pass
        at = Attention()
        for j in range(QUAD):
            for t in range(NT):
                at.maximum(0, j, t, result[0], result[1])
        at.max_rows(0)
        finish(*at.mrow_free[0], *(Point(f"store_{i}", "start", q.total(f"store_{i}", "start"), 16) for i in range(2)))

        region("first", False, True)
        region("middle", True, True)
        region("last", True, False)
        q.enter("tail")
        ring.reset()
        points = {}
        for _ in stage_c(0, points):
            pass
        finish(points["out"])

        q.region = "setup"
        q.put("sp", lambda e, b: e.nop())
        q.put("pe", lambda e, b: e.transpose(psum[:, 0, 0:P], ident[:], ident[:]), consts)
        q.put("act", lambda e, b: e.activation(gate[:, 0:1], onecol[:], ACT.Copy), consts)
        streams = sorted({s for s, _ in q.counts})
        sems = {s: sem("s_" + s) for s in streams}
        block = ctx.enter_context(nc.Block())
        order = [("setup", 1), ("start", 1), ("first", 1), ("middle", B - 2), ("last", 1), ("tail", 1)]

        def run(engine):
            def issue(e, name, b, base, in_loop):
                seen = {}
                for other in ENGINES if name != "setup" else ():
                    e.wait_ge(sems[other], base(other))
                    e.nop(nofuse=True)
                for fn, waits, point in q.items[engine].get(name, []):
                    new = False
                    for w in waits:
                        if seen.get((w.sem_name, w.region), 0) >= w.count:
                            continue
                        assert w.region in (name, "setup")
                        seen[(w.sem_name, w.region)] = w.count
                        new = True
                        e.wait_ge(sems[w.sem_name], w.count + (base(w.sem_name) if w.region == name else 0))
                        if in_loop and engine == "sp":
                            e.nop(nofuse=True)
                    if in_loop and new and engine != "sp":
                        e.nop(nofuse=True)
                    ins = fn(e, b)
                    ins.then_inc(sems[point.sem_name], point.unit)

            def body(e):
                done = {s: 0 for s in streams}
                batch = 0
                for name, times in order:
                    if times == 1:
                        issue(e, name, batch, lambda s: done[s], False)
                    else:
                        with e.Fori(0, times) as i:
                            held = {}

                            def base(s, i=i, held=held):
                                if s not in held:
                                    held[s] = e.snap(i * q.total(s, name) + done[s])
                                return held[s]

                            issue(e, name, i + batch, base, True)
                    for s in streams:
                        done[s] += times * q.total(s, name)
                    if name in ("first", "middle"):
                        batch += times
            return body

        block.sync(run("sp"))
        block.gpsimd(run("pool"))
        block.scalar(run("act"))
        block.vector(run("dve"))
        block.tensor(run("pe"))


_SHORT = {"x": "x", "ctx_1024": "ctx_1024"}
_PREFIXES = ("L0_xattn_", "L0_ffn_mha_", "L0_ffn_")


def _short(name):
    for p in _PREFIXES:
        if name.startswith(p):
            return name[len(p):]
    return name


def kernel(**inputs):
    import concourse.bacc as _bacc
    from concourse.bass_utils import run_bass_kernel_spmd as _run

    nc = _bacc.Bacc("TRN2", target_bir_lowering=False, num_devices=1)
    arrays, d = {}, {}
    for name in inputs:
        a = np.ascontiguousarray(inputs[name])
        arrays[f"in_{name}"] = a
        d[_short(name)] = nc.dram_tensor(f"in_{name}", a.shape, mybir.dt.from_np(a.dtype), kind="ExternalInput").ap()
    shape = inputs["x"].shape
    out = nc.dram_tensor("out", shape, F32, kind="ExternalOutput").ap()
    build(nc, d, out)
    r = _run(nc, [arrays], core_ids=[0])
    return r.results[0]["out"]
```

```python
from contextlib import ExitStack

import numpy as np
import concourse.bass as bass
from concourse import mybir

F32 = mybir.dt.float32
BF16 = mybir.dt.bfloat16
U32 = mybir.dt.uint32
ALU = mybir.AluOpType
ACT = mybir.ActivationFunctionType
AX = mybir.AxisListType.X

P = 128
ENGINES = ("pe", "act", "dve", "pool", "sp")


class Point:

    def __init__(self, sem_name, region, count, unit):
        self.sem_name, self.region, self.count, self.unit = sem_name, region, count, unit




class Queues:

    def __init__(self):
        self.items = {e: {} for e in ENGINES}
        self.counts = {}
        self.region = None

    def enter(self, region):
        self.region = region

    def _point(self, sem_name, unit):
        key = (sem_name, self.region)
        self.counts[key] = self.counts.get(key, 0) + unit
        return Point(sem_name, self.region, self.counts[key], unit)

    def put(self, engine, fn, *waits):
        point = self._point(engine, 1)
        self.items[engine].setdefault(self.region, []).append((fn, [w for w in waits if w is not None], point))
        return point

    def dma(self, engine, stream, fn, *waits):
        point = self._point(stream, 16)
        self.items[engine].setdefault(self.region, []).append((fn, [w for w in waits if w is not None], point))
        return point

    def total(self, sem_name, region):
        return self.counts.get((sem_name, region), 0)


class Stage:

    def __init__(self, pieces, pause):
        self.pieces, self.pause, self.left, self.over = pieces, pause, 0, False

    def tick(self):
        if self.left == 0 and not self.over:
            try:
                self.left = next(self.pieces) or self.pause
            except StopIteration:
                self.over = True
        self.left -= 1
        return not self.over

    def rest(self):
        for _ in self.pieces:
            pass
        self.over = True


class Banks:

    def __init__(self, banks):
        self.banks, self.busy, self.order = banks, {b: () for b in banks}, list(banks)

    def take(self):
        bank = self.order.pop(0)
        return bank, self.busy[bank]

    def free(self, bank, *points):
        self.busy[bank] = points
        self.order.append(bank)

    def reset(self):
        assert len(self.order) == len(self.banks)
        self.busy = {b: () for b in self.banks}


def build(nc, d, out):
    B, S, E = d["x"].shape
    NT = S // P
    KC = E // P
    NH = d["ig_bias"].shape[0]
    DH = E // NH
    NG = NH * NT
    M, _, H, KD = d["wq"].shape
    HC = P // KD
    NX = d["ffn_rb"].shape[0]
    FF = d["fw1"].shape[2]
    FC = FF // P
    TOPK = 2
    QUAD = 4
    NQ = M * H // QUAD
    TERMS_K = (0, 0, 1, 1, 0, 2)
    TERMS_Q = (0, 1, 0, 1, 2, 0)
    KROWS = len(TERMS_K) * KD
    VW = KD + 1

    q = Queues()
    ctx = ExitStack()
    with ctx:
        def sb(name, shape, dt=F32):
            return ctx.enter_context(nc.sbuf_tensor(name, shape, dt))

        psum = ctx.enter_context(nc.psum_tensor("psum", [P, 8, 512], F32))

        ident = sb("ident", [P, P])
        onecol = sb("onecol", [P, 1])
        neghalf = sb("neghalf", [P, NG])
        wgate = sb("wgate", [P, 3 * KC, 2, NH])
        wgkv = sb("wgkv", [P, KC, 2, NH])
        gbias = sb("gbias", [NH, 2])
        onw = sb("onw", [P, E])
        ln1 = sb("ln1", [P, 2, KC])
        ln2 = sb("ln2", [P, 2, KC])
        wq = sb("wq", [P, KC, M, H * KD])
        wk = sb("wk", [P, KC, M, H * KD])
        wv = sb("wv", [P, KC, M, H * KD])
        bq = sb("bq", [P, M, KC])
        bqs = sb("bqs", [P, M, KC])
        bk = sb("bk", [P, M, KC])
        bv = sb("bv", [P, M, H * KD])
        wo = sb("wo", [P, M, KC, E])
        bo = sb("bo", [P, M, E])
        rw = sb("rw", [P, KC, M])
        rb = sb("rb", [P, M])
        fr = sb("fr", [P, KC, NX])
        fb = sb("fb", [P, NX])

        xin = sb("xin", [P, NT, E])
        kin = sb("kin", [P, NT, E])
        vaug = sb("vaug", [P, NT, NH, DH + 1])
        qbuf = sb("qbuf", [P, NG * (DH + 1)])
        qn = qbuf[:, 0:NT * E].rearrange("p (t n) -> p t n", t=NT)
        num = qbuf[:].rearrange("p (c h n) -> p c h n", c=NT, h=NH)
        qT = sb("qT", [P, KC, S])
        kT = sb("kT", [P, KC, S])
        hh = qT[:].rearrange("p c (g d) -> p (c g) d", d=DH)
        hs = kT[:].rearrange("p c (g d) -> p (c g) d", d=DH)
        proj = sb("proj", [P, 2, S])
        resid = sb("resid", [P, 2, S])
        gi, gf = proj[0:NH, 0], proj[0:NH, 1]
        ga, lf = resid[0:NH, 0], resid[0:NH, 1]
        AW = NH * (DH + 1)
        vdec = resid[:].rearrange("p a s -> p (a s)")[:, 0:(NT - 1) * AW].rearrange(
            "p (c h n) -> p c h n", c=NT - 1, h=NH)
        flat = proj[:].rearrange("p a s -> p (a s)")
        inter = flat[:, 0:AW].rearrange("p (h n) -> p h n", h=NH)
        state = flat[:, AW:AW + (NT - 1) * AW // 2].rearrange("p (c h n) -> p c h n", c=NT - 1, h=NH // 2)
        parts = sb("parts", [P, 2, 3, S], BF16)
        rows = parts[0:NH].rearrange("p a j s -> p (a j s)").bitcast(F32).rearrange("p (r s) -> p r s", r=3)
        cols = sb("cols", [P, 3, NT, NH])
        gend = sb("gend", [P, NH, NT])
        dec = sb("dec", [P, 4, NT, NH])
        cmat = sb("cmat", [P, NH, S])
        nrm = sb("nrm", [P, 2, NG])
        hm = sb("hm", [P, 4, NG])
        n1T = sb("n1T", [P, KC, S])
        mp = sb("mp", [P, M])
        kst = sb("kst", [P, M * H, S], BF16)
        qst = sb("qst", [P, M * H, S], BF16)
        vst = sb("vst", [P, NT, M * H, VW])
        mpc = sb("mpc", [P, M])
        mx = sb("mx", [P, M * H, NT])
        mrow = sb("mrow", [QUAD * NT, 2, 2, P], BF16)
        prob = sb("prob", [P, 2, QUAD, S])
        ctxs = sb("ctxs", [P, S])
        rden = sb("rden", [P, NT, QUAD])
        cx = sb("cx", [P, NT, M, H * KD])
        x2k = sb("x2k", [P, NT, E])
        mk = sb("mk", [P, 2, NT])
        bmix = sb("bmix", [P, E])
        x3 = sb("x3", [P, NT, E])
        acc = sb("acc", [P, NT, E])
        cxT = sb("cxT", [P, M, KC, S])
        hT = cxT[:].rearrange("p m c s -> p (m c) s")
        n2T = sb("n2T", [P, KC, S])
        w1 = x3[:].rearrange("p t n -> p (t n)").rearrange("p (c f) -> p c f", c=KC)
        w2 = sb("w2", [P, FC, E])
        ep = sb("ep", [P, NX])
        top = sb("top", [P, NX])
        topi = sb("topi", [P, NX], U32)
        gate = sb("gate", [P, TOPK])

        class Scratch:

            def __init__(self, tag):
                self.stats = sb("stats" + tag, [P, NT, 6])
                self.mv = sb("mv" + tag, [P, NT, 2])
                self.rstd = sb("rstd" + tag, [P, 4, NT])
                self.msum = sb("msum" + tag, [P, KC])
                self.mbc = sb("mbc" + tag, [P, KC, P])
                self.sm = sb("sm" + tag, [P, 4])

        sa, se = Scratch("_a"), Scratch("_e")
        G_dram = nc.dram_tensor("G_dram", (NH, S), F32, kind="Internal").ap()
        parts_dram = nc.dram_tensor("parts_dram", (2, M, KC, 3, P, S), BF16, kind="Internal").ap()

        def sem(name):
            return ctx.enter_context(nc.semaphore(name))

        q.enter("setup")

        def load(stream, dst, src):
            return q.dma("sp", stream, lambda e, b: e.dma_start(dst, src, allow_slow_non_contiguous=True))

        ldk0 = load("first_ctx", kin[:], d["ctx_1024"][0].rearrange("(t p) n -> p t n", p=P))
        ldx0 = load("first_x", xin[:], d["x"][0].rearrange("(t p) n -> p t n", p=P))

        for g, name in enumerate(("ig_kernel", "fg_kernel")):
            load("w_gates", wgate[:, :, g, :], d[name].rearrange("(c p) h -> p c h", p=P))
            gates_in = load("w_gates", gbias[:, g:g + 1], d[("ig_bias", "fg_bias")[g]].rearrange("(h o) -> h o", o=1))
        load("weights", onw[:], d["outnorm_weight"].rearrange("(o h) d -> o (h d)", o=1).to_broadcast([P, E]))
        for i, t in enumerate((ln1, ln2)):
            for j, s in enumerate("gb"):
                load("weights", t[:, j, :], d[f"ln{i + 1}_{s}"].rearrange("(c p) -> p c", p=P))
        for t, name in ((wq, "wq"), (wk, "wk"), (wv, "wv")):
            for m in range(M):
                load("weights", t[:, :, m, :], d[name][m].rearrange("(c p) h k -> p c (h k)", p=P))
        for t, name in ((bq, "bq"), (bk, "bk")):
            for m in range(M):
                load("weights", t[:, m, :], d[name][m].rearrange("(c h) k -> (h k) c", c=KC))
        load("weights", bv[:], d["bv"].rearrange("(o m) h k -> o m (h k)", o=1).to_broadcast([P, M, H * KD]))
        for m in range(M):
            load("weights", wo[:, m, :, :], d["wo"][m].rearrange("(c h) k n -> (h k) c n", c=KC))
        load("weights", bo[:], d["bo"].rearrange("(o m) n -> o m n", o=1).to_broadcast([P, M, E]))
        load("weights", rw[:], d["rw"].rearrange("(c p) m -> p c m", p=P))
        load("weights", rb[:], d["rb"].rearrange("(o m) -> o m", o=1).to_broadcast([P, M]))
        load("weights", fr[:], d["ffn_rw"].rearrange("(c p) m -> p c m", p=P))
        weights = load("weights", fb[:], d["ffn_rb"].rearrange("(o m) -> o m", o=1).to_broadcast([P, NX]))

        zero = q.put("pool", lambda e, b: e.memset(ident[:], 0.0))
        q.put("pool", lambda e, b: e.affine_select(out=ident[:], in_=ident[:], compare_op=ALU.not_equal, fill=1.0,
                                                   base=0, pattern=[[-1, P]], channel_multiplier=1), zero)
        q.put("pool", lambda e, b: e.memset(onecol[:], 1.0))
        q.put("pool", lambda e, b: e.memset(neghalf[:], -0.5))
        q.put("pool", lambda e, b: e.memset(vaug[:, :, :, DH:DH + 1], 1.0))
        consts = q.put("pool", lambda e, b: e.memset(vst[:, :, :, KD:KD + 1], 1.0))
        q.put("dve", lambda e, b: e.memset(kst[KROWS:KROWS + 2, :, :], 1.0))
        q.put("dve", lambda e, b: e.memset(psum[:, 6, :], 0.0))
        q.put("dve", lambda e, b: e.tensor_tensor(wgkv[:], wgate[:, KC:2 * KC], wgate[:, 2 * KC:3 * KC], ALU.add),
              gates_in)

        def mm(out_, lhsT, rhs, start, stop, *waits, **kw):
            return q.put("pe", lambda e, b: e.matmul(out_, lhsT, rhs, start=start, stop=stop, **kw), *waits)

        def tr(out_, in_, n, *waits):
            return q.put("pe", lambda e, b: e.transpose(out_, in_, ident[0:n, 0:n]), *waits)

        def act(out_, in_, f, *waits, **kw):
            return q.put("act", lambda e, b: e.activation(out_, in_, f, **kw), *waits)

        def tt(eng, out_, a, c, op, *waits):
            return q.put(eng, lambda e, b: e.tensor_tensor(out_, a, c, op), *waits)

        def ts(eng, out_, a, s1, s2, op0, op1, *waits):
            if op1 is None:
                return q.put(eng, lambda e, b: e.tensor_scalar(out_, a, s1, None, op0), *waits)
            return q.put(eng, lambda e, b: e.tensor_scalar(out_, a, s1, s2, op0, op1), *waits)

        def stt(out_, a, s, c, op0, op1, *waits):
            return q.put("dve", lambda e, b: e.scalar_tensor_tensor(out=out_, in0=a, scalar=s, in1=c,
                                                                    op0=op0, op1=op1), *waits)

        def red(out_, in_, op, *waits):
            return q.put("dve", lambda e, b: e.tensor_reduce(out_, in_, AX, op), *waits)

        def copy(eng, out_, in_, *waits):
            return q.put(eng, lambda e, b: e.tensor_copy(out_, in_), *waits)

        def power(out_, in_, n, *waits):
            return q.put("pool", lambda e, b: e.tensor_tensor(out_, in_, neghalf[:, 0:n], ALU.pow), *waits)

        ring = Banks((5, 7, 4))

        def moments(sc, src, *waits):
            for t in range(NT):
                a = q.put("dve", lambda e, b, t=t: e.bn_stats(sc.stats[:, t, :], src[:, t, :]), *waits)
                if t == 1:
                    yield 1
            for t in range(NT):
                last = q.put("dve", lambda e, b, t=t: e.bn_aggr(sc.mv[:, t, :], sc.stats[:, t, :]), a)
            return last

        def chunk_to_columns(src, c, evacuate, *waits):
            bk_, free = ring.take()
            for t in range(NT):
                last = tr(psum[:, bk_, t * P:(t + 1) * P], src[:, t, c * P:(c + 1) * P], P, *waits, *free)
            done = evacuate(c, psum[:, bk_, :], last)
            ring.free(bk_, done)
            return done

        def mean_columns(sc, *done):
            s_ = ts("dve", sc.msum[:], sc.msum[:], 1.0 / S, None, ALU.mult, None, *done)
            return copy("dve", sc.mbc[:], sc.msum[:].unsqueeze(2).to_broadcast([P, KC, P]), s_)

        def logits(sc, dst, w_, bias_, n, bcd):
            br, free = ring.take()
            for c in range(KC):
                w = mm(psum[:, br, 0:n], sc.mbc[:, c, :], w_[:, c, :], c == 0, c == KC - 1, bcd, *free)
            p1 = tt("dve", dst[:], psum[:, br, 0:n], bias_[:], ALU.add, w)
            ring.free(br, p1)
            return p1

        def softmax(sc, v, p1):
            p2 = red(sc.sm[:, 0:1], v[:], ALU.max, p1)
            p3 = ts("dve", v[:], v[:], sc.sm[:, 0:1], None, ALU.subtract, None, p2)
            p4 = act(v[:], v[:], ACT.Exp, p3)
            p5 = red(sc.sm[:, 1:2], v[:], ALU.add, p4)
            p6 = q.put("dve", lambda e, b: e.reciprocal(sc.sm[:, 2:3], sc.sm[:, 1:2]), p5)
            return ts("dve", v[:], v[:], sc.sm[:, 2:3], None, ALU.mult, None, p6)

        def stage_a(ahead, late, x_free, n1T_free, stack_free, vst_free, result, fill=lambda: None):
            ldk = ldk0 if ahead == 0 else q.dma("sp", "load_ctx", lambda e, b: e.dma_start(
                kin[:], d["ctx_1024"][bass.ds(b + ahead, 1)].rearrange("o (t p) n -> p (o t) n", p=P)))
            yield
            kTd = []
            for c in range(KC):
                kTd.append(chunk_to_columns(kin, c, lambda c, ps, w: act(kT[:, c, :], ps, ACT.Copy, w), ldk))
                yield
            while x_free and not x_free[0]:
                yield
            ldx = ldx0 if ahead == 0 else q.dma("sp", "load_x", lambda e, b: e.dma_start(
                xin[:], d["x"][bass.ds(b + ahead, 1)].rearrange("o (t p) n -> p (o t) n", p=P)), *(x_free or ()))
            yield 3
            mo = yield from moments(sa, xin, ldx)
            e1 = ts("dve", sa.rstd[:, 0, :], sa.mv[:, :, 1], 1e-5, None, ALU.add, None, mo)
            pw = power(sa.rstd[:, 1, :], sa.rstd[:, 0, :], NT, e1)
            vcopy = copy("pool", vaug[:, :, :, 0:DH], kin[:].rearrange("p t (h d) -> p t h d", h=NH), ldk)
            yield 3
            for t in range(NT):
                qdone = ts("dve", qn[:, t, :], xin[:, t, :], sa.mv[:, t, 0:1], sa.rstd[:, 1, t:t + 1],
                           ALU.subtract, ALU.mult, pw)
                if t == 1:
                    yield 1
            yield 1
            qTd = []
            for c in range(KC):
                qTd.append(chunk_to_columns(qn, c, lambda c, ps, w: act(qT[:, c, :], ps, ACT.Copy, w), qdone))
                yield

            bk_, free = ring.take()
            for t in range(NT):
                for c in range(2 * KC):
                    src = (kT if c < KC else qT)[:, c % KC, t * P:(t + 1) * P]
                    w_ = (wgkv if c < KC else wgate)[:, c % KC].rearrange("p g h -> p (g h)")
                    last = mm(psum[:, bk_, t * 2 * NH:(t + 1) * 2 * NH], src, w_, c == 0, c == 2 * KC - 1,
                              *kTd, *qTd, *free)
            gcol = cols[:].rearrange("p r c h -> p (r c h)")[:, 0:2 * NG]
            gcd = copy("dve", gcol, psum[:, bk_, 0:2 * NG], last)
            ring.free(bk_, gcd)
            yield 1

            def gate_row(g, dst):
                bk_, free = ring.take()
                for t in range(NT):
                    o = (t * 2 + g) * NH
                    last = tr(psum[0:NH, bk_, t * P:(t + 1) * P], gcol[:, o:o + NH], P, gcd, *free)
                done = act(dst, psum[0:NH, bk_, :], ACT.Identity, last, bias=gbias[:, g:g + 1])
                ring.free(bk_, done)
                return done

            fgd = gate_row(1, gf)
            igd = gate_row(0, gi)
            yield 1
            a1 = stt(ga, gf, -1.0, gf, ALU.mult, ALU.min, fgd)
            a2 = act(ga, ga, ACT.Exp, a1)
            a3 = act(ga, ga, ACT.Ln, a2, bias=onecol[0:NH, :])
            fill()
            yield
            lfd = stt(lf, gf, 0.0, ga, ALU.min, ALU.subtract, a3)
            Fd = q.put("dve", lambda e, b: e.tensor_tensor_scan(gf, onecol[0:NH].to_broadcast([NH, S]), lf, 0.0, ALU.mult, ALU.add), lfd)
            gd = tt("dve", rows[:, 0, :], gi, gf, ALU.subtract, Fd, igd)
            yield
            Gd = q.put("dve", lambda e, b: e.tensor_tensor_scan(rows[:, 1, :], rows[:, 0, :], rows[:, 0, :], -3.0e38,
                                                                ALU.max, ALU.max), gd)
            Gst = q.dma("sp", "store_G", lambda e, b: e.dma_start(G_dram, rows[:, 1, :]), Gd)
            Gbc = q.dma("sp", "load_G", lambda e, b: e.dma_start(
                cmat[:], G_dram.rearrange("(o h) s -> o h s", o=1).to_broadcast([P, NH, S])), Gst)
            Md = tt("dve", rows[:, 2, :], gf, rows[:, 1, :], ALU.add, Gd)
            yield

            bc, free = ring.take()
            for r in range(3):
                for c in range(NT):
                    o = (r * NT + c) * NH
                    last = tr(psum[:, bc, o:o + NH], rows[:, r, c * P:(c + 1) * P], NH, Md, *free)
            cold = copy("dve", cols[:].rearrange("p r c h -> p (r c h)"), psum[:, bc, 0:3 * NG], last)
            ring.free(bc, cold)
            yield
            yield 1
            fill()
            yield 1
            gends = [copy("dve", gend[:], cmat[:, :, P - 1::P], Gbc)]
            masked = []
            for h in range(NH):
                for c in range(NT):
                    v = cmat[:, h, c * P:(c + 1) * P]
                    last = act(v, v, ACT.Exp, Gbc, cold, *gends, bias=cols[:, 0, c, h:h + 1], scale=-1.0)
                dview = cmat[:, h, :].rearrange("p (c s) -> p c s", c=NT)
                masked.append(q.put("pool", lambda e, b, v=dview: e.affine_select(
                    out=v, in_=v, compare_op=ALU.is_ge, fill=0.0, base=0, pattern=[[0, NT], [1, P]],
                    channel_multiplier=-1), last))
                yield 1

            ge = gend[:].rearrange("p h c -> p c h")
            tt("dve", dec[:, 0, 1:NT, :], ge[:, 0:NT - 1, :], cols[:, 1, 1:NT, :], ALU.subtract, *gends, cold)
            tt("dve", dec[:, 1, 0:NT - 1, :], cols[:, 0, 0:NT - 1, :], ge[:, 0:NT - 1, :], ALU.subtract)
            tt("dve", dec[:, 2, 1:NT - 1, :], ge[:, 0:NT - 2, :], ge[:, 1:NT - 1, :], ALU.subtract)
            dd = ts("dve", dec[:, 3, :, :], cols[:, 2, :, :], -1.0, None, ALU.mult, None)
            yield 1
            act(dec[:, 0, 1:NT, :], dec[:, 0, 1:NT, :], ACT.Exp, dd)
            act(dec[:, 1, 0:NT - 1, :], dec[:, 1, 0:NT - 1, :], ACT.Exp)
            act(dec[:, 2, 1:NT - 1, :], dec[:, 2, 1:NT - 1, :], ACT.Exp)
            decd = act(dec[:, 3, :, :], dec[:, 3, :, :], ACT.Exp)
            wsc = ts("dve", dec[:, 1, 0:NT - 1, :], dec[:, 1, 0:NT - 1, :], DH ** -0.5, None, ALU.mult, None, decd)
            vw = tt("pool", vdec, vaug[:, 0:NT - 1],
                    dec[:, 1, 0:NT - 1, :].unsqueeze(3).to_broadcast([P, NT - 1, NH, DH + 1]), ALU.mult, wsc, vcopy)
            yield

            cd = []
            for h in range(NH):
                ba, free = ring.take()
                o = DH * (h % 2)
                for c in range(NT):
                    s_ = slice(c * P, (c + 1) * P)
                    last = mm(psum[:, ba, s_], kT[o:o + DH, h // 2, s_], qT[o:o + DH, h // 2, s_], True, True,
                              *qTd, *kTd, *free)
                yield 1
                cd.append(stt(cmat[:, h, :], psum[:, ba, :], DH ** -0.5, cmat[:, h, :], ALU.mult, ALU.mult, last,
                              masked[h]))
                ring.free(ba, cd[-1])
                yield 1

            st = None
            for c in range(NT - 1):
                if c:
                    yield 1
                bs, free = ring.take()
                for h in range(NH):
                    o = DH * (h % 2)
                    last = mm(psum[o:o + DH, bs, (h // 2) * (DH + 1):(h // 2 + 1) * (DH + 1)],
                              kin[:, c, h * DH:(h + 1) * DH], vdec[:, c, h, :], True, True, vw, *free)
                yield 1
                if c == 0:
                    st = copy("dve", state[:, 0, :, :].rearrange("p a n -> p (a n)"),
                              psum[:, bs, 0:(NH // 2) * (DH + 1)], last)
                else:
                    prev = st
                    for h in range(NH):
                        o = DH * (h % 2)
                        st = stt(state[o:o + DH, c, h // 2, :], state[o:o + DH, c - 1, h // 2, :],
                                 dec[o:o + DH, 2, c, h:h + 1],
                                 psum[o:o + DH, bs, (h // 2) * (DH + 1):(h // 2 + 1) * (DH + 1)],
                                 ALU.mult, ALU.add, last, prev, decd)
                ring.free(bs, st)

            numd = []
            for c in range(NT):
                s_ = slice(c * P, (c + 1) * P)
                bn, free = ring.take()
                for h in range(NH):
                    wi_ = mm(psum[:, bn, h * (DH + 1):(h + 1) * (DH + 1)], cmat[:, h, s_], vaug[:, c, h, :], True, True,
                             *cd, vcopy, *free)
                intra = psum[:, bn, 0:NH * (DH + 1)].rearrange("p (h n) -> p h n", h=NH)
                if c == 0:
                    numd.append(copy("dve", num[:, c], intra, wi_))
                else:
                    t1 = []
                    for par in range(2):
                        bx, free = ring.take()
                        o = DH * par
                        for hp in range(NH // 2):
                            wx = mm(psum[:, bx, hp * (DH + 1):(hp + 1) * (DH + 1)], qT[o:o + DH, hp, s_],
                                    state[o:o + DH, c - 1, hp, :], True, True, st, *free)
                        t1.append(tt("dve", inter[:, par::2, :],
                                     psum[:, bx, 0:NH // 2 * (DH + 1)].rearrange("p (h n) -> p h n", n=DH + 1),
                                     dec[:, 0, c, par::2].unsqueeze(2).to_broadcast([P, NH // 2, DH + 1]), ALU.mult,
                                     wx, decd, *numd[-1:]))
                        ring.free(bx, t1[-1])
                    numd.append(tt("dve", num[:, c], intra, inter, ALU.add, *t1, wi_))
                ring.free(bn, numd[-1])
                yield

            numf = num.rearrange("p c h n -> p (c h) n")
            n_ = act(nrm[:, 1, :], numf[:, :, DH], ACT.Abs, *numd)
            n0 = tt("dve", nrm[:, 0, :], nrm[:, 1, :], dec[:, 3].rearrange("p c h -> p (c h)"), ALU.max, n_, decd)
            n1_ = ts("dve", nrm[:, 0, :], nrm[:, 0, :], 1e-6, None, ALU.add, None, n0)
            n2_ = q.put("dve", lambda e, b: e.reciprocal(nrm[:, 1, :], nrm[:, 0, :]), n1_)

            def over_head(v):
                return v.unsqueeze(2).to_broadcast([P, NG, DH])

            hd = tt("dve", hh, numf[:, :, 0:DH], over_head(nrm[:, 1, :]), ALU.mult, n2_)
            yield 1
            m1 = red(hm[:, 0, :], hh, ALU.add, hd)
            m2 = ts("dve", hm[:, 0, :], hm[:, 0, :], 1.0 / DH, None, ALU.mult, None, m1)
            yield
            hc = tt("dve", hh, hh, over_head(hm[:, 0, :]), ALU.subtract, m2)
            yield 2
            sq = act(hs, hh, ACT.Square, hc)
            yield 2
            v1 = red(hm[:, 1, :], hs, ALU.add, sq)
            v2 = ts("dve", hm[:, 2, :], hm[:, 1, :], 1.0 / DH, 1e-6, ALU.mult, ALU.add, v1)
            v3 = power(hm[:, 3, :], hm[:, 2, :], NG, v2)
            hv = hh.rearrange("p (c h) n -> p c (h n)", c=NT)
            hw = tt("dve", hs.rearrange("p (c h) n -> p c (h n)", c=NT), hv,
                    onw[:].unsqueeze(1).to_broadcast([P, NT, E]), ALU.mult, v1, *late)
            yield 2
            hn = tt("dve", hh, hs, over_head(hm[:, 3, :]), ALU.mult, v3, hw)
            yield
            x2d = tt("dve", xin[:], xin[:], hv, ALU.add, hn)
            yield 2

            mo = yield from moments(sa, xin, x2d)
            r0 = ts("dve", sa.rstd[:, 0, :], sa.mv[:, :, 1], 1e-5, None, ALU.add, None, mo)
            r1 = power(sa.rstd[:, 1, :], sa.rstd[:, 0, :], NT, r0)
            yield 2
            r2 = tt("dve", sa.rstd[:, 2, :], sa.mv[:, :, 1], sa.rstd[:, 1, :], ALU.mult, r1)
            r3 = tt("dve", sa.rstd[:, 2, :], sa.rstd[:, 2, :], sa.rstd[:, 1, :], ALU.mult, r2)
            r4 = ts("dve", sa.rstd[:, 2, :], sa.rstd[:, 2, :], 1e-6, None, ALU.add, None, r3)
            r5 = power(sa.rstd[:, 3, :], sa.rstd[:, 2, :], NT, r4)
            r6 = tt("pool", sa.rstd[:, 3, :], sa.rstd[:, 3, :], sa.rstd[:, 1, :], ALU.mult, r5)
            yield 2
            for t in range(NT):
                n1d = ts("dve", qn[:, t, :], xin[:, t, :], sa.mv[:, t, 0:1], sa.rstd[:, 3, t:t + 1],
                         ALU.subtract, ALU.mult, r6)
                if t == 1:
                    yield 1
            yield 1
            n1Td = []
            for c in range(KC):
                n1Td.append(chunk_to_columns(qn, c, lambda c, ps, w: act(
                    n1T[:, c, :], ps, ACT.Identity, w, *n1T_free, *late, scale=ln1[:, 0, c:c + 1], bias=ln1[:, 1, c:c + 1],
                    accum_out=sa.msum[:, c:c + 1]), n1d))
                yield

            if late:
                n1Td.append(ts("dve", bqs[:], bq[:], KD ** -0.5, None, ALU.mult, None, *late))

            slot_free = [None, None]
            n = 0
            for m in range(M):
                for which, (w_, bias_, scale_) in enumerate(((wk, bk, 1.0), (wq, bqs, KD ** -0.5))):
                    sts = []
                    for c in range(KC):
                        sl = n % 2
                        n += 1
                        bp, free = ring.take()
                        for kc in range(KC):
                            w = mm(psum[:, bp, :], w_[:, kc, m, c * P:(c + 1) * P], n1T[:, kc, :], kc == 0, kc == KC - 1,
                                   *n1Td, *late, *free)
                        f1 = act(proj[:, sl, :], psum[:, bp, :], ACT.Identity, w, slot_free[sl], bias=bias_[:, m, c:c + 1],
                                 scale=scale_)
                        f2 = act(parts[:, sl, 0, :], psum[:, bp, :], ACT.Identity, w, slot_free[sl],
                                 bias=bias_[:, m, c:c + 1], scale=scale_)
                        ring.free(bp, f2)
                        yield 1
                        g2 = tt("dve", resid[:, sl, :], proj[:, sl, :], parts[:, sl, 0, :], ALU.subtract, f1, f2)
                        g3 = copy("dve", parts[:, sl, 1, :], resid[:, sl, :], g2)
                        g4 = tt("dve", parts[:, sl, 2, :], resid[:, sl, :], parts[:, sl, 1, :], ALU.subtract, g3)
                        slot_free[sl] = q.dma("sp", f"store_{sl}", lambda e, b, m=m, c=c, sl=sl, which=which: e.dma_start(
                            parts_dram[which, m, c].rearrange("j p s -> p j s"), parts[:, sl, :, :]), g4)
                        sts.append(slot_free[sl])
                        yield 1
                    if m == 0:
                        while stack_free and not stack_free[0]:
                            yield
                        result[which] = load_stack(which, 0, *sts, *(stack_free or ()))
                if m == 0:
                    while vst_free and not vst_free[0]:
                        yield
                    for pt in range(NT // 2):
                        project_v(0, pt, *n1Td, *(vst_free or ()))
                        yield
                    bcd = mean_columns(sa, *n1Td)
                    yield
                    p1 = logits(sa, mp, rw, rb, M, bcd)
                    softmax(sa, mp, p1)
                    yield

        def load_stack(which, m, *waits):
            for i, j in enumerate((TERMS_K, TERMS_Q)[which]):
                for c in range(KC):
                    ld = q.dma("sp", f"stack_{which}_{m}", lambda e, b, c=c, i=i, j=j: e.dma_start(
                        (kst, qst)[which][i * KD:(i + 1) * KD, m * H + c * HC:m * H + (c + 1) * HC, :],
                        parts_dram[which, m, c, j].rearrange("(h k) s -> k h s", k=KD)), *waits)
            return ld

        def project_v(m, pt, *waits):
            bvb, free = ring.take()
            for i in range(2):
                t = 2 * pt + i
                for kc in range(KC):
                    w = mm(psum[:, bvb, i * H * KD:(i + 1) * H * KD], n1T[:, kc, t * P:(t + 1) * P], wv[:, kc, m, :],
                           kc == 0, kc == KC - 1, *waits, *free)
            v_ = psum[:, bvb, :].rearrange("p (t h k) -> p t h k", t=2, k=KD)
            for i in range(2):
                vd = tt("dve", vst[:, 2 * pt + i, m * H:(m + 1) * H, 0:KD], v_[:, i],
                        bv[:, m].rearrange("p (h k) -> p h k", k=KD), ALU.add, w)
            ring.free(bvb, vd)
            return w, vd

        def stage_c(behind, points):
            for t in range(NT):
                xfd = ts("dve", x3[:, t, :], x2k[:, t, :], mk[:, 0, t:t + 1], mk[:, 1, t:t + 1], ALU.subtract, ALU.mult)
            x3a = tt("dve", x3[:], x3[:], bmix[:].unsqueeze(1).to_broadcast([P, NT, E]), ALU.add, xfd)
            points["bmix_read"] = x3a
            acc0 = tt("pool", acc[:], x3[:], x2k[:], ALU.add, x3a)
            points["x2k_read"] = acc0
            cxTd = []
            for m in range(M):
                for c in range(KC):
                    cxTd.append(chunk_to_columns(cx[:, :, m, :], c, lambda c, ps, w, m=m: act(
                        cxT[:, m, c, :], ps, ACT.Copy, w)))
            points["cx_read"] = cxTd[-1]
            yield
            for t in range(NT):
                bw, free = ring.take()
                k = 0
                for m in range(M):
                    for c in range(KC):
                        w = mm(psum[:, bw, 0:E], cxT[:, m, c, t * P:(t + 1) * P], wo[:, m, c, :], k == 0,
                               k == M * KC - 1, *cxTd, *free)
                        k += 1
                x3d = tt("dve", x3[:, t, :], x3[:, t, :], psum[:, bw, 0:E], ALU.add, w, acc0)
                accd = tt("dve", acc[:, t, :], acc[:, t, :], psum[:, bw, 0:E], ALU.add, w, acc0)
                ring.free(bw, accd)
                yield 2
            wo_read = w
            mo = yield from moments(se, x3, x3d)
            r0 = ts("dve", se.rstd[:, 0, :], se.mv[:, :, 1], 1e-6, None, ALU.add, None, mo)
            r1 = power(se.rstd[:, 1, :], se.rstd[:, 0, :], NT, r0)
            yield
            for t in range(NT):
                n2d = ts("dve", x3[:, t, :], x3[:, t, :], se.mv[:, t, 0:1], se.rstd[:, 1, t:t + 1],
                         ALU.subtract, ALU.mult, r1)
                if t == 1:
                    yield 1
            yield 1
            n2Td = []
            for c in range(KC):
                n2Td.append(chunk_to_columns(x3, c, lambda c, ps, w: act(
                    n2T[:, c, :], ps, ACT.Identity, w, scale=ln2[:, 0, c:c + 1], bias=ln2[:, 1, c:c + 1],
                    accum_out=se.msum[:, c:c + 1]), n2d))
                yield
            bcd = mean_columns(se, *n2Td)
            yield
            p1 = logits(se, ep, fr, fb, NX, bcd)
            p4 = softmax(se, ep, p1)
            yield
            p5 = q.put("dve", lambda e, b: e.max(top[:], ep[:]), p4)
            topd = q.put("dve", lambda e, b: e.max_index(topi[:], top[:], ep[:]), p5)
            p6 = red(se.sm[:, 3:4], top[:, 0:TOPK], ALU.add, p5)
            p7 = q.put("dve", lambda e, b: e.reciprocal(se.sm[:, 3:4], se.sm[:, 3:4]), p6)
            gated = ts("dve", gate[:], top[:, 0:TOPK], se.sm[:, 3:4], None, ALU.mult, None, p7)
            yield 6

            def fetch(k, tag, dst, src, *waits):
                def fn(e, b):
                    x_ = e.value_load(topi[0:1, k:k + 1], min_val=0, max_val=NX - 1)
                    return e.dma_start(dst[:], src[bass.ds(x_, 1)].rearrange("o (c p) n -> p (o c) n", p=P))
                return q.dma("sp", f"expert_{tag}", fn, topd, *waits)

            w1d = fetch(0, "w1", w1, d["fw1"], *n2Td)
            w2d = fetch(0, "w2", w2, d["fw2"])
            yield 8
            hfree = (wo_read,)
            for k in range(TOPK):
                hd_ = []
                def hidden(f, *waits):
                    bh, free = ring.take()
                    for kc in range(KC):
                        w = mm(psum[:, bh, :], w1[:, kc, f * P:(f + 1) * P], n2T[:, kc, :], kc == 0, kc == KC - 1,
                               w1d, *n2Td, *free)
                    return bh, w

                for f in range(FC // 2):
                    bh, w = hidden(f)
                    hcd = copy("dve", hT[:, f, :], psum[:, bh, :], w, *hfree)
                    ring.free(bh, hcd)
                    yield 3
                hd_.append(act(hT[:, 0:FC // 2, :], hT[:, 0:FC // 2, :], ACT.Gelu, hcd))
                rest = [hidden(f) for f in range(FC // 2, FC)]
                for f, (bh, w) in zip(range(FC // 2, FC), rest):
                    hd_.append(act(hT[:, f, :], psum[:, bh, :], ACT.Gelu, w, *hfree))
                    ring.free(bh, hd_[-1])
                if k + 1 < TOPK:
                    w1d = fetch(k + 1, "w1", w1, d["fw1"], w)
                yield
                for t in range(NT):
                    be, free = ring.take()
                    for f in range(FC):
                        w = mm(psum[:, be, 0:E], hT[:, f, t * P:(t + 1) * P], w2[:, f, :], f == 0, f == FC - 1,
                               *hd_, w2d, *free)
                    yield 1
                    accd = stt(acc[:, t, :], psum[:, be, 0:E], gate[:, k:k + 1], acc[:, t, :], ALU.mult, ALU.add,
                               w, gated, accd)
                    ring.free(be, accd)
                    yield 2
                hfree = (w,)
                if k + 1 < TOPK:
                    w2d = fetch(k + 1, "w2", w2, d["fw2"], w)
            points["out"] = q.dma("sp", "store_out", lambda e, b: e.dma_start(
                out[bass.ds(b - behind, 1)].rearrange("o (t p) n -> p (o t) n", p=P), acc[:]), accd)

        class Attention:
            def __init__(self):
                self.sc_free, self.sm_free = [(), ()], [(), ()]
                self.cx_free, self.pr_free, self.cs_free, self.rd_free = (), [(), ()], (), ()
                self.mrow_free = [(), ()]
                self.tile_n = self.sm_n = 0
                self.mxd, self.rowd, self.expd, self.scored = {}, {}, {}, {}

            def maximum(self, qq, j, t, *waits):
                h = qq % NQ * QUAD + j
                i = self.sm_n % 2
                self.sm_n += 1
                w = mm(psum[:, 2 + i, :], qst[0:KROWS, h, t * P:(t + 1) * P], kst[0:KROWS, h, :], True, True,
                       *waits, *self.sm_free[i])
                r = red(mx[:, h, t:t + 1], psum[:, 2 + i, :], ALU.max, w)
                self.sm_free[i] = (r,)
                self.mxd[qq] = r

            def max_rows(self, qq):
                n = qq % NQ
                bk_, free = ring.take()
                src = psum[0:QUAD * NT, bk_, 0:P]
                w = tr(src, mx[:, n * QUAD:(n + 1) * QUAD, :].rearrange("p h t -> p (h t)"), P, self.mxd[qq], *free)
                i = qq % 2
                a = ts("dve", mrow[:, i, 0, :], src, -1.0, None, ALU.mult, None, w, *self.mrow_free[i])
                c_ = stt(mrow[:, i, 1, :], src, -1.0, mrow[:, i, 0, :], ALU.mult, ALU.subtract, a)
                ring.free(bk_, c_)
                self.mrow_done = c_

            def send_rows(self, qq, *waits):
                n, i = qq % NQ, qq % 2
                for r in range(2):
                    ld = q.dma("act", f"rows_{i}", lambda e, b, r=r: e.dma_start(
                        qst[KROWS + r:KROWS + r + 1, n * QUAD:(n + 1) * QUAD, :], mrow[:, i, r, :]),
                        self.mrow_done, *waits)
                self.mrow_free[i] = (ld,)
                self.rowd[qq] = ld

            def score(self, qq, g, j):
                sl = g % 2
                i = self.tile_n % 2
                self.tile_n += 1
                h = qq * QUAD + j
                w = mm(psum[:, i, :], kst[0:KROWS + 2, h, g * P:(g + 1) * P], qst[0:KROWS + 2, h, :],
                       True, True, self.rowd.get(qq), *self.sc_free[i])
                x_ = act(prob[:, sl, j, :], psum[:, i, :], ACT.Exp, w, *self.pr_free[sl])
                self.sc_free[i] = (x_,)
                self.expd[(qq, g)] = x_
                self.scored[qq] = w

            def values(self, qq, g, *waits):
                sl = g % 2
                for j in range(QUAD):
                    h = qq * QUAD + j
                    w = mm(psum[32 * j:32 * j + VW, 6, :], vst[:, g, h, :], prob[:, sl, j, :], g == 0, g == NT - 1,
                           self.expd[(qq, g)], *waits, *(self.cx_free if g == 0 else ()), tile_position=(0, 32 * j))
                self.pr_free[sl] = (w,)
                return w

            def copy_context(self, w):
                self.copied = act(ctxs[:], psum[:, 6, :], ACT.Copy, w, *self.cs_free)
                self.cx_free = (self.copied,)

            def context(self, qq, *waits):
                m = qq * QUAD // H
                bk_, free = ring.take()
                for t in range(NT):
                    w = tr(psum[:, bk_, t * P:(t + 1) * P], ctxs[:, t * P:(t + 1) * P], P, self.copied, *free)
                self.cs_free = (w,)
                v = psum[:, bk_, :].rearrange("p (t j n) -> p t j n", t=NT, j=QUAD)
                r = q.put("dve", lambda e, b: e.reciprocal(rden[:], v[:, :, :, KD]), w, *self.rd_free)
                o = (qq * QUAD) % H * KD
                c_ = stt(cx[:, :, m, o:o + QUAD * KD].rearrange("p t (j k) -> p t j k", k=KD), v[:, :, :, 0:KD],
                         mpc[:, m:m + 1], rden[:].unsqueeze(3).to_broadcast([P, NT, QUAD, KD]), ALU.mult, ALU.mult,
                         r, *waits)
                self.rd_free = (c_,)
                ring.free(bk_, c_)

        def finish(*points):
            q.put("sp", lambda e, b: e.nop(), *points)

        LEAD = 3

        def region(name, with_c, with_a):
            q.enter(name)
            ring.reset()
            at = Attention()
            points, result = {}, {}
            n1T_free = []
            mpd = copy("dve", mpc[:], mp[:])
            output = Stage(stage_c(1, points) if with_c else iter(()), 3)

            def carry():
                c1 = act(x2k[:], xin[:], ACT.Copy, points.get("x2k_read"))
                copy("pool", mk[:, 0, :], sa.mv[:, :, 0], points.get("x2k_read"))
                c2 = copy("pool", mk[:, 1, :], sa.rstd[:, 1, :])
                b0 = ts("dve", bmix[:], bo[:, 0, :], mpc[:, 0:1], None, ALU.mult, None, mpd, points.get("bmix_read"))
                stt(bmix[:], bo[:, 1, :], mpc[:, 1:2], bmix[:], ALU.mult, ALU.add, b0)
                return c1, c2

            def second_values():
                for pt in range(NT // 2):
                    w, points["v1"] = project_v(1, pt)
                    yield
                n1T_free.append(w)

            a_waits = {"x": [], "stack": [], "vst": []}
            values2 = Stage(second_values(), 4)
            values2.left = 10 * QUAD if with_a and with_c else 0

            def fill():
                if with_c:
                    values2.left = 0
                    values2.tick()
                    values2.left = 10 * QUAD

            inputs = Stage(stage_a(1, (), a_waits["x"], n1T_free, a_waits["stack"], a_waits["vst"], result, fill)
                           if with_a else iter(()), 2)
            inputs.tick()
            s1 = [load_stack(which, 1) for which in range(2)]

            if with_a:
                a_waits["x"].append(None)
                a_waits["stack"].append(None)
                a_waits["vst"].append(None)
            if with_c:
                output.tick()
                output.left = 2
            tile = 0
            for qq in range(NQ):
                for g in range(NT):
                    slot = qq * NT + g
                    for j in range(QUAD):
                        at.score(qq, g, j)
                        for _ in range(2 if slot < LEAD and j % 2 == 0 else 1):
                            if tile < (NQ - 1) * QUAD * NT:
                                ahead = 1 + tile // (QUAD * NT)
                                at.maximum(ahead, tile // NT % QUAD, tile % NT, *(s1 if ahead >= NQ // 2 else ()))
                                tile += 1
                        if qq == NQ - 1 and with_a:
                            at.maximum(NQ, g, j, result[0], result[1])
                        if g == LEAD and j == 0 and qq + 1 < NQ:
                            at.send_rows(qq + 1)
                        values2.tick()
                        output.tick()
                        if slot == 0 and j == QUAD - 1:
                            a_waits["x"][:] = carry()
                        inputs.tick()
                    if g > 0:
                        at.values(qq, g - 1, *((points["v1"],) if qq >= NQ // 2 else ()))
                    elif qq > 0:
                        w = at.values(qq - 1, NT - 1)
                        at.copy_context(w)
                    if g == 1 and qq > 0:
                        at.context(qq - 1, points.get("cx_read"), mpd)
                    if g == LEAD - 1 and qq + 1 < NQ:
                        at.max_rows(qq + 1)
                    if with_a and slot == NQ // 2 * NT:
                        a_waits["stack"][0] = at.scored[NQ // 2 - 1]
                        a_waits["vst"][0] = w
                if qq == NQ - 2 and with_a:
                    while inputs.tick() and (0 not in result or 1 not in result):
                        inputs.left = 0
            if with_a:
                at.max_rows(NQ)
                at.send_rows(NQ, a_waits["stack"][0])
            w = at.values(NQ - 1, NT - 1, points["v1"])
            at.copy_context(w)
            at.context(NQ - 1, points.get("cx_read"), mpd)
            output.rest()
            inputs.rest()
            finish(points.get("out"), *at.mrow_free[0], *at.mrow_free[1], *s1,
                   *(Point(f"store_{i}", name, q.total(f"store_{i}", name), 16) for i in range(2) if with_a))

        q.enter("start")
        result = {}
        for _ in stage_a(0, (weights,), [], [], [], [], result):
            pass
        at = Attention()
        for j in range(QUAD):
            for t in range(NT):
                at.maximum(0, j, t, result[0], result[1])
        at.max_rows(0)
        at.send_rows(0)
        finish(*at.mrow_free[0], *(Point(f"store_{i}", "start", q.total(f"store_{i}", "start"), 16) for i in range(2)))

        region("first", False, True)
        region("middle", True, True)
        region("last", True, False)
        q.enter("tail")
        ring.reset()
        points = {}
        for _ in stage_c(0, points):
            pass
        finish(points["out"])

        q.region = "setup"
        q.put("sp", lambda e, b: e.nop())
        q.put("pe", lambda e, b: e.transpose(psum[:, 0, 0:P], ident[:], ident[:]), consts)
        q.put("act", lambda e, b: e.activation(gate[:, 0:1], onecol[:], ACT.Copy), consts)
        streams = sorted({s for s, _ in q.counts})
        sems = {s: sem("s_" + s) for s in streams}
        block = ctx.enter_context(nc.Block())
        order = [("setup", 1), ("start", 1), ("first", 1), ("middle", B - 2), ("last", 1), ("tail", 1)]

        def run(engine):
            def issue(e, name, b, base, in_loop):
                seen = {}
                for other in ENGINES if name != "setup" else ():
                    e.wait_ge(sems[other], base(other))
                    e.nop(nofuse=True)
                for fn, waits, point in q.items[engine].get(name, []):
                    new = False
                    for w in waits:
                        if seen.get((w.sem_name, w.region), 0) >= w.count:
                            continue
                        assert w.region in (name, "setup")
                        seen[(w.sem_name, w.region)] = w.count
                        new = True
                        e.wait_ge(sems[w.sem_name], w.count + (base(w.sem_name) if w.region == name else 0))
                        if in_loop and engine == "sp":
                            e.nop(nofuse=True)
                    if in_loop and new and engine != "sp":
                        e.nop(nofuse=True)
                    ins = fn(e, b)
                    ins.then_inc(sems[point.sem_name], point.unit)

            def body(e):
                done = {s: 0 for s in streams}
                batch = 0
                for name, times in order:
                    if times == 1:
                        issue(e, name, batch, lambda s: done[s], False)
                    else:
                        with e.Fori(0, times) as i:
                            held = {}

                            def base(s, i=i, held=held):
                                if s not in held:
                                    held[s] = e.snap(i * q.total(s, name) + done[s])
                                return held[s]

                            issue(e, name, i + batch, base, True)
                    for s in streams:
                        done[s] += times * q.total(s, name)
                    if name in ("first", "middle"):
                        batch += times
            return body

        block.sync(run("sp"))
        block.gpsimd(run("pool"))
        block.scalar(run("act"))
        block.vector(run("dve"))
        block.tensor(run("pe"))


_SHORT = {"x": "x", "ctx_1024": "ctx_1024"}
_PREFIXES = ("L0_xattn_", "L0_ffn_mha_", "L0_ffn_")


def _short(name):
    for p in _PREFIXES:
        if name.startswith(p):
            return name[len(p):]
    return name


def kernel(**inputs):
    import concourse.bacc as _bacc
    from concourse.bass_utils import run_bass_kernel_spmd as _run

    nc = _bacc.Bacc("TRN2", target_bir_lowering=False, num_devices=1)
    arrays, d = {}, {}
    for name in inputs:
        a = np.ascontiguousarray(inputs[name])
        arrays[f"in_{name}"] = a
        d[_short(name)] = nc.dram_tensor(f"in_{name}", a.shape, mybir.dt.from_np(a.dtype), kind="ExternalInput").ap()
    shape = inputs["x"].shape
    out = nc.dram_tensor("out", shape, F32, kind="ExternalOutput").ap()
    build(nc, d, out)
    r = _run(nc, [arrays], core_ids=[0])
    return r.results[0]["out"]
```
